# Optimizing a Trainium2 kernel written in Bass

```python
import numpy as np
import jax
import jax.numpy as jnp

def _softmax(x, axis=-1):
    return jax.nn.softmax(x, axis=axis)

def _gelu(x):
    return jax.nn.gelu(x, approximate=True)

def _silu(x):
    return jax.nn.silu(x)

def _sigmoid(x):
    return jax.nn.sigmoid(x)

def _layernorm(x, axis=-1, eps=1e-05):
    m = jnp.mean(x, axis=axis, keepdims=True)
    v = jnp.var(x, axis=axis, keepdims=True)
    return (x - m) / jnp.sqrt(v + eps)

def _scatter_add(tgt, idx, src, axis=0):
    return tgt.at[idx].add(src)

def _segment_sum(src, seg, n):
    return jax.ops.segment_sum(src, seg, n)
kernel_name = 'mk_adaln_d1_jaxref_r8_b3495e'

def setup_inputs(seed: int=0):
    np.random.seed(seed)
    _w = jnp.asarray

    def _L0_attn_setup():
        import jax, jax.numpy as jnp
        import numpy as np
        NUM_GROUPS = 8
        key = jax.random.key(seed)
        k1, k2, k3, k4 = jax.random.split(key, 4)
        B, S, D = (1, 512, 128)
        hidden_states = jax.random.normal(k1, (B, S, D), dtype=jnp.float32)
        Wq = jax.random.normal(k2, (D, D), dtype=jnp.float32) * D ** (-0.5)
        Wk = jax.random.normal(k3, (D, D), dtype=jnp.float32) * D ** (-0.5)
        Wv = jax.random.normal(k4, (D, D), dtype=jnp.float32) * D ** (-0.5)
        return {'hidden_states': hidden_states, 'Wq': Wq, 'Wk': Wk, 'Wv': Wv}
    _L0_attn_in = _L0_attn_setup()

    def _L0_ffn_setup():
        import jax, jax.numpy as jnp
        import numpy as np
        TOP_P = 0.3
        key = jax.random.key(seed)
        k1, k2, k3, k4 = jax.random.split(key, 4)
        B, S, D, H, E = (4, 512, 128, 128, 8)
        x = jax.random.normal(k1, (B, S, D), dtype=jnp.float32)
        gate_W = jax.random.normal(k2, (E, D), dtype=jnp.float32) / np.float32(np.sqrt(D))
        expert_W = jax.random.normal(k3, (E, H, D), dtype=jnp.float32) / np.float32(np.sqrt(D))
        out_W = jax.random.normal(k4, (D, H), dtype=jnp.float32) / np.float32(np.sqrt(H))
        return {'x': x, 'gate_W': gate_W, 'expert_W': expert_W, 'out_W': out_W}
    _L0_ffn_in = _L0_ffn_setup()
    _L0_c = _w((lambda *s: np.random.randn(*s).astype(np.float32) * 0.05)(1, 128))
    _L0_wmod = _w((lambda *s: np.random.randn(*s).astype(np.float32) * 0.05)(128, 6 * 128) * 128 ** (-0.5))
    _d = {'L0_attn_hidden_states': _L0_attn_in['hidden_states'], 'L0_attn_Wq': _L0_attn_in['Wq'], 'L0_attn_Wk': _L0_attn_in['Wk'], 'L0_attn_Wv': _L0_attn_in['Wv'], 'L0_ffn_gate_W': _L0_ffn_in['gate_W'], 'L0_ffn_expert_W': _L0_ffn_in['expert_W'], 'L0_ffn_out_W': _L0_ffn_in['out_W'], 'L0_c': _L0_c, 'L0_wmod': _L0_wmod}
    _x0 = _d['L0_attn_hidden_states']
    _d['L0_attn_hidden_states'] = jax.random.normal(jax.random.fold_in(jax.random.key(seed), 1), (1, 2048, 128), dtype=_x0.dtype)
    del _x0
    return _d

def reference(L0_attn_hidden_states, L0_attn_Wq, L0_attn_Wk, L0_attn_Wv, L0_ffn_gate_W, L0_ffn_expert_W, L0_ffn_out_W, L0_c, L0_wmod):

    def _L0_attn_ref(hidden_states, Wq, Wk, Wv):
        import jax, jax.numpy as jnp
        import numpy as np
        NUM_GROUPS = 8
        B, S, D = hidden_states.shape
        H = NUM_GROUPS
        hd = D // H
        scale = hd ** 0.5
        q = (hidden_states @ Wq.T).reshape(B, S, H, hd).transpose(0, 2, 1, 3)
        k = (hidden_states @ Wk.T).reshape(B, S, H, hd).transpose(0, 2, 1, 3)
        v = (hidden_states @ Wv.T).reshape(B, S, H, hd).transpose(0, 2, 1, 3)
        scores = jnp.einsum('bhqd,bhkd->bhqk', q, k) / scale
        causal = jnp.tril(jnp.ones((S, S), dtype=bool))
        scores = jnp.where(causal[None, None], scores, jnp.float32(-jnp.inf))
        probs = jax.nn.softmax(scores, axis=-1)
        context = jnp.einsum('bhqk,bhkd->bhqd', probs, v)
        context = context.transpose(0, 2, 1, 3).reshape(B, S, D)
        return context

    def _L0_ffn_ref(x, gate_W, expert_W, out_W):
        import jax, jax.numpy as jnp
        import numpy as np
        TOP_P = 0.3
        B, S, D = x.shape
        E = gate_W.shape[0]
        N = B * S
        p = jax.nn.softmax(jnp.einsum('bsd,ed->bse', x, gate_W), axis=-1).reshape(N, E)
        tpi = (p > TOP_P).astype(jnp.int32)
        cnt = jnp.sum(tpi[:, :, None] == jnp.arange(E)[None, None, :], axis=1)
        scale = cnt.astype(x.dtype) * p
        x2 = x.reshape(N, D)
        h = jnp.einsum('nd,ehd->neh', x2, expert_W)
        final = jnp.einsum('neh,ne->nh', h, scale)
        out = jnp.einsum('nh,dh->nd', final, out_W).reshape(B, S, D)
        return out
    x = L0_attn_hidden_states
    mod = (_silu(L0_c) @ L0_wmod).reshape(L0_c.shape[0], 6, 1, -1)
    sa, ca, ga, sb, cb, gb = (mod[:, 0], mod[:, 1], mod[:, 2], mod[:, 3], mod[:, 4], mod[:, 5])
    ga = (2 * (ga >= 0) - 1) * jnp.maximum(jnp.abs(ga), 0.25)
    gb = (2 * (gb >= 0) - 1) * jnp.maximum(jnp.abs(gb), 0.25)
    h = _layernorm(x, axis=-1) * (1 + ca) + sa
    x = x + ga * _L0_attn_ref(h, L0_attn_Wq, L0_attn_Wk, L0_attn_Wv)
    h = _layernorm(x, axis=-1) * (1 + cb) + sb
    x = x + gb * _L0_ffn_ref(h, L0_ffn_gate_W, L0_ffn_expert_W, L0_ffn_out_W)
    return x

_drawn_inputs = setup_inputs


def setup_inputs(seed=0):
    import zlib

    import numpy as np

    out = dict(_drawn_inputs(seed))
    spreads = {}
    factors = {}
    for name, (base, spread) in spreads.items():
        noise = np.random.default_rng([zlib.crc32(name.encode()), seed]).standard_normal(out[name].shape)
        drawn = base * np.exp(spread * noise) if base else spread * noise
        out[name] = jnp.asarray(drawn.astype(out[name].dtype))
    for name, factor in factors.items():
        out[name] = (out[name] * factor).astype(out[name].dtype)
    return out
```

```python
from contextlib import ExitStack

import concourse.bass as bass
from concourse import mybir

F32 = mybir.dt.float32
BF16 = mybir.dt.bfloat16
ALU = mybir.AluOpType
ACT = mybir.ActivationFunctionType
AX = mybir.AxisListType

P = 128
S, D = 2048, 128
NH = 8
HD = D // NH
NE = 8
TOP_P = 0.3
EPS = 1e-5
GATE_FLOOR = 0.25
NT = S // P
TG = 4
GROUP = TG * P
NG = S // GROUP
HALF = 4
NI = 2 * NG
VW = 32
MAIN = 3 * HD
SCORE_SCALE = HD ** -0.5
MASKED = -(2.0 ** 100)
ACT_RING, VEC_RING = 3, 2
PROB_BUFS = 4
PV_LAG = 2
BANK = 512

IN_ACT_RING = {"weights", "ffn_weights", "norm_t", "values", "max_t", "scores", "norm2_t", "logits"}
IN_VEC_RING = {"modulation", "expert_out", "project", "maxima", "context_t", "ffn"}


def item_batches():
    return [(n, j) for n in range(NI) for j in range(TG * (n // 2) + TG)]


def plan():
    steps = [("stats", 0), ("weights",), ("modulation",), ("normalize", 0), ("norm_t", 0), ("project", 0),
             ("ffn_weights",), ("expert_out",), ("values", 0)]
    batches = item_batches()
    first = {}
    for b, (n, j) in enumerate(batches):
        first.setdefault(n, b)
    units = []
    for n in range(NI):
        g = n // 2
        units.append([("maxima", n, i, e, c) for i in range(TG) for e in range(HALF // 2) for c in range(g + 1)])

    def prepare(g):
        return [[("stats", g)], [("normalize", g), ("norm_t", g)], [("project", g), ("values", g)]]

    lead = 3
    due = {n: max(0, first[n] - lead) for n in range(NI)}
    queue = []
    extra = {b: [] for b in range(len(batches) + 16)}
    steps += sum(prepare(1), []) + units[0] + [("max_sum", 0), ("max_t", 0)]
    at = {2: 0, 3: first[2]}
    for g in range(2, NG):
        for k, s in enumerate(prepare(g)):
            extra[at[g] + k] += s
    todo = [(n, u) for n in range(1, NI) for u in units[n]]
    done = 0
    needed = {n: sum(len(units[m]) for m in range(1, n + 1)) for n in range(1, NI)}
    owed = 0.0
    pending = []
    for b, (n, j) in enumerate(batches):
        for s in extra[b]:
            steps.append(s)
        rate = max([(needed[m] - done) / max(1, due[m] - b) for m in range(1, NI) if needed[m] > done] or [0])
        owed += rate
        take = []
        while owed >= 1 - 1e-9 and done < len(todo):
            m, u = todo[done]
            if ("project", m // 2) not in steps:
                break
            take.append(u)
            done += 1
            owed -= 1
            if done == needed[m]:
                take += [("max_sum", m), ("max_t", m)]
        k = (len(take) + 1) // 2
        steps += [("scores", b, 0), ("scores", b, 1)] + take[:k] + [("scores", b, 2), ("scores", b, 3)] + take[k:]
        steps += [s for s in pending if s[0] <= b and steps.extend(s[1])] and []
        pending = [s for s in pending if s[0] > b]
        if b >= PV_LAG:
            steps.append(("probs_v", b - PV_LAG))
            m, jj = batches[b - PV_LAG]
            if jj == TG * (m // 2) + TG - 1:
                pending += finish(m, b)
    for b in range(len(batches) - PV_LAG, len(batches)):
        steps.append(("probs_v", b))
    pending += finish(NI - 1, len(batches))
    for s in sorted(pending, key=lambda s: s[0]):
        steps += s[1]
    return steps


def finish(n, b):
    out = [(b, [("context", n)]), (b + 1, [("context_t", n)])]
    if n % 2:
        g = n // 2
        out += [(b + 1, [("stats2", g)]), (b + 2, [("normalize2", g), ("norm2_t", g)]), (b + 3, [("logits", g)]),
                (b + 4, [("gate", g)]), (b + 5, [("ffn", g)])]
    return out


def block_kernel(nc, x_in, wq_in, wk_in, wv_in, gate_w_in, expert_w_in, out_w_in, c_in, wmod_in, out):
    steps = plan()
    batches = item_batches()
    last_batch = {n: b for b, (n, _) in enumerate(batches)}
    act_slot = {s: k for k, s in enumerate([s for s in steps if s[0] in IN_ACT_RING])}
    vec_slot = {s: k for k, s in enumerate([s for s in steps if s[0] in IN_VEC_RING])}
    diagonal = [b for b, (n, j) in enumerate(batches) if j >= TG * (n // 2)]

    def first_query(b):
        n, j = batches[b]
        return max(0, j - TG * (n // 2)) * P

    def masks_until(b):
        return sum(1 for d in diagonal if d <= b)

    with ExitStack() as ctx:
        def sb(name, shape, dt):
            return ctx.enter_context(nc.sbuf_tensor(name, shape, dt))

        def sem(name):
            return ctx.enter_context(nc.semaphore(name))

        act_ps = ctx.enter_context(nc.psum_tensor("act_ps", [P, ACT_RING, BANK], F32))
        vec_ps = ctx.enter_context(nc.psum_tensor("vec_ps", [P, VEC_RING, 2, BANK], F32))
        ctx_ps = ctx.enter_context(nc.psum_tensor("ctx_ps", [P, BANK], F32))

        x_sb = sb("x_sb", [P, NT, D], F32)
        w_sb = sb("w_sb", [P, 4, D], F32)
        w_t = sb("w_t", [P, 3, D], F32)
        wv_gated = sb("wv_gated", [P, D], F32)
        out_w_t = sb("out_w_t", [P, D], F32)
        gate_w = sb("gate_w", [NE, D], F32)
        gate_w_t = sb("gate_w_t", [P, NE], F32)
        expert_w = sb("expert_w", [P, 2, D], F32)
        ffn_w = sb("ffn_w", [P, 2, D], F32)
        c_col = sb("c_col", [P, 1], F32)
        silu = sb("silu", [P, 4], F32)
        silu_wide = sb("silu_wide", [P, P], F32)
        wmod = sb("wmod", [P, 6, D], F32)
        mod_col = sb("mod_col", [P, 4], F32)
        gates = sb("gates", [P, 2, D], F32)
        gate_raw = sb("gate_raw", [P, 2, D], F32)
        gate_sign = sb("gate_sign", [P, 2, D], F32)
        gate_size = sb("gate_size", [P, 2, D], F32)
        ident = sb("ident", [P, P], F32)
        ident_bf = sb("ident_bf", [P, P], BF16)
        mask = sb("mask", [P, P], BF16)
        ones = sb("ones", [P, P], F32)
        ones_row = sb("ones_row", [2, S], BF16)
        half_neg = sb("half_neg", [P, TG], F32)
        bn = sb("bn", [P, TG, 6], F32)
        mean_var = sb("mean_var", [P, 2, TG, 2], F32)
        var_eps = sb("var_eps", [P, 2, TG], F32)
        rstd = sb("rstd", [P, 2, TG], F32)
        normed = sb("normed", [P, 2, TG, D], F32)
        h_t = sb("h_t", [P, S], F32)
        piece = [sb(f"piece{k}", [P, 2, S], BF16) for k in range(3)]
        left = sb("left", [P, 2, 2, GROUP], F32)
        q_stack = sb("q_stack", [P, NH, S], BF16)
        k_stack = sb("k_stack", [P, NH, S], BF16)
        v_aug = sb("v_aug", [P, NT, NH, VW], F32)
        part_max = sb("part_max", [P, 2, TG, 2, 2, NG], F32)
        neg_max = sb("neg_max", [P, TG * HALF], F32)
        max_piece = sb("max_piece", [P, 2, TG, 2, 2, 2], BF16)
        max_row = sb("max_row", [8, 2, GROUP], BF16)
        probs = sb("probs", [P, PROB_BUFS, HALF, GROUP], F32)
        ctx_t = sb("ctx_t", [P, 2, GROUP], F32)
        ctx_norm = sb("ctx_norm", [P, TG, HALF * HD], F32)
        sum_inv = sb("sum_inv", [P, TG, HALF], F32)
        h2_t = sb("h2_t", [P, GROUP], F32)
        logits = sb("logits", [P, TG, NE], F32)
        top = sb("top", [P, TG], F32)
        shifted = sb("shifted", [P, TG, NE], F32)
        gate_e = sb("gate_e", [P, TG, NE], F32)
        gate_sum = sb("gate_sum", [P, TG], F32)
        gate_inv = sb("gate_inv", [P, TG], F32)
        gate_p = sb("gate_p", [P, TG, NE], F32)
        flags = sb("flags", [P, TG, NE], F32)
        count = sb("count", [P, TG, 2], F32)
        expert_scale = sb("expert_scale", [P, TG, 2], F32)
        ffn_part = sb("ffn_part", [P, TG, D], F32)
        result = sb("result", [P, 2, TG, D], F32)

        scratch = nc.dram_tensor("piece_scratch", (3, 2, D, S), BF16, kind="Internal").ap()

        x_in_sem = [sem(f"x_in{g}") for g in range(NG)]
        w_in = sem("w_in")
        mod_in = sem("mod_in")
        expert_in = sem("expert_in")
        const_ready = sem("const_ready")
        ones_in = sem("ones_in")
        act_filled = sem("act_filled")
        act_drained = sem("act_drained")
        vec_filled = sem("vec_filled")
        vec_drained = sem("vec_drained")
        vec_order = sem("vec_order")
        exp_c = sem("exp_c")
        silu_ready = sem("silu_ready")
        gates_ready = sem("gates_ready")
        wv_ready = sem("wv_ready")
        var_ready = sem("var_ready")
        rstd_ready = sem("rstd_ready")
        pool_order = sem("pool_order")
        norm_ready = sem("norm_ready")
        piece_ready = [sem(f"piece_ready{k}") for k in range(3)]
        stored = [sem(f"stored{g}") for g in range(NG)]
        stored_lo = [sem(f"stored_lo{g}") for g in range(NG)]
        main_in = [sem(f"main_in{g}") for g in range(NG)]
        rest_in = [sem(f"rest_in{g}") for g in range(NG)]
        max_ready = sem("max_ready")
        max_in = [sem(f"max_in{n}") for n in range(NI)]
        masked = sem("masked")
        pv_done = sem("pv_done")
        ctx_copied = sem("ctx_copied")
        shift_ready = sem("shift_ready")
        gate_exp = sem("gate_exp")
        out_stored = [sem(f"out_stored{g}") for g in range(NG)]

        CONSTS = dict(ident=2, ident_bf=4, mask=6, ones=7, half_neg=8, ones_row=9, v_zero=10, v_one=11)
        N_MAIN = 2 * 3 * 2
        N_REST = 2 * (3 + 4)
        norms = [s for s in steps if s[0] in ("stats", "stats2")]
        norm_no = {s: k for k, s in enumerate(norms)}

        main_rows = [(0, 0), (0, 1), (1, 0)]
        rest_rows = {0: [(1, 1), (0, 2), (2, 0)], 1: [(1, 1), (0, 2), (2, 0), (1, 2)]}
        main_at = {0: 0, 1: 64}
        rest_at = {0: MAIN + 2, 1: 0}
        stack_rows = {0: 2 * MAIN + 2, 1: 64 + MAIN + 2}

        x_tiles = x_in.rearrange("b (t p) d -> p (b t) d", p=P)
        out_tiles = out.rearrange("b (t p) d -> p (b t) d", p=P)

        block = ctx.enter_context(nc.Block())

        @block.sync
        def _(sp):
            sp.dma_start(x_sb[:, 0:TG, :], x_tiles[:, 0:TG, :]).then_inc(x_in_sem[0], 16)
            sp.dma_start(c_col[:, :], c_in.rearrange("a d -> d a")).then_inc(mod_in, 16)
            sp.dma_start(wmod[:, :, :], wmod_in.rearrange("d (s n) -> d s n", s=6)).then_inc(mod_in, 16)
            for k, w in enumerate((wq_in, wk_in, wv_in, out_w_in)):
                sp.dma_start(w_sb[:, k, :], w).then_inc(w_in, 16)
            sp.dma_start(gate_w[:, :], gate_w_in).then_inc(w_in, 16)
            sp.dma_start(expert_w[:, :, :], expert_w_in[0:2].rearrange("e h d -> h e d")).then_inc(expert_in, 16)
            for g in range(1, NG):
                sp.dma_start(x_sb[:, TG * g:TG * g + TG, :],
                             x_tiles[:, TG * g:TG * g + TG, :]).then_inc(x_in_sem[g], 16)
            sp.wait_ge(const_ready, CONSTS["ones_row"])
            for h in range(NH):
                r = main_at[h % 2] + MAIN
                sp.dma_start(k_stack[r:r + 2, h, :], ones_row[:, :]).then_inc(ones_in, 16)

            def stack(qk, piece_no, row, odd, cols, done):
                dst = (q_stack, k_stack)[qk][row:row + HD, odd::2, cols]
                src = scratch[piece_no, qk, :, cols].rearrange("(e t p) c -> t p e c", t=2, p=HD)[odd]
                sp.dma_start(dst, src).then_inc(done, 16)

            for step in steps:
                if step[0] == "project":
                    g = step[1]
                    cols = slice(g * GROUP, (g + 1) * GROUP)
                    for k in range(2):
                        sp.wait_ge(piece_ready[k], g + 1)
                        sp.dma_start(scratch[k, :, :, cols].rearrange("a p c -> p a c"),
                                     piece[k][:, :, cols]).then_inc(stored[g], 16)
                    sp.wait_ge(stored[g], 32)
                    for odd in range(2):
                        for r, pieces in enumerate(main_rows):
                            for qk in range(2):
                                stack(qk, pieces[qk], main_at[odd] + r * HD, odd, cols, main_in[g])
                    sp.wait_ge(piece_ready[2], g + 1)
                    sp.dma_start(scratch[2, :, :, cols].rearrange("a p c -> p a c"),
                                 piece[2][:, :, cols]).then_inc(stored_lo[g], 16)
                    sp.wait_ge(stored_lo[g], 16)
                    for odd in range(2):
                        for r, pieces in enumerate(rest_rows[odd]):
                            for qk in range(2):
                                stack(qk, pieces[qk], rest_at[odd] + r * HD, odd, cols, rest_in[g])
                elif step[0] == "max_t":
                    n = step[1]
                    g, first = n // 2, HALF * (n % 2)
                    sp.wait_ge(act_drained, act_slot[step] + 1)
                    for odd in range(2):
                        for a in range(2):
                            r = main_at[odd] + MAIN + a
                            sp.dma_start(q_stack[r:r + 1, first + odd:first + HALF:2, g * GROUP:(g + 1) * GROUP],
                                         max_row[4 * odd + 2 * a:4 * odd + 2 * a + 2, n % 2, :]).then_inc(max_in[n], 16)
                elif step[0] == "ffn":
                    g = step[1]
                    sp.wait_ge(vec_drained, vec_slot[step] + 1)
                    sp.dma_start(out_tiles[:, TG * g:TG * g + TG, :], result[:, g % 2]).then_inc(out_stored[g], 16)
            for g in range(NG):
                sp.wait_ge(out_stored[g], 16)

        @block.gpsimd
        def _(pool):
            pool.memset(ident[:, :], 0.0).then_inc(const_ready, 1)
            pool.wait_ge(const_ready, 1)
            pool.affine_select(out=ident[:, :], in_=ident[:, :], compare_op=ALU.not_equal, fill=1.0, base=0,
                               pattern=[[-1, P]], channel_multiplier=1).then_inc(const_ready, 1)
            pool.memset(ident_bf[:, :], 0.0).then_inc(const_ready, 1)
            pool.wait_ge(const_ready, 3)
            pool.affine_select(out=ident_bf[:, :], in_=ident_bf[:, :], compare_op=ALU.not_equal, fill=1.0, base=0,
                               pattern=[[-1, P]], channel_multiplier=1).then_inc(const_ready, 1)
            pool.memset(mask[:, :], 0.0).then_inc(const_ready, 1)
            pool.wait_ge(const_ready, 5)
            pool.affine_select(out=mask[:, :], in_=mask[:, :], compare_op=ALU.is_ge, fill=MASKED, base=0,
                               pattern=[[-1, P]], channel_multiplier=1).then_inc(const_ready, 1)
            pool.memset(ones[:, :], 1.0).then_inc(const_ready, 1)
            pool.memset(half_neg[:, :], -0.5).then_inc(const_ready, 1)
            pool.memset(ones_row[:, :], 1.0).then_inc(const_ready, 1)
            pool.memset(v_aug[:, :, :, :], 0.0).then_inc(const_ready, 1)
            pool.wait_ge(const_ready, CONSTS["v_zero"])
            pool.memset(v_aug[:, :, :, HD:HD + 1], 1.0).then_inc(const_ready, 1)

            for step in steps:
                if step[0] in ("stats", "stats2"):
                    k = norm_no[step]
                    pool.wait_ge(var_ready, k + 1)
                    pool.tensor_tensor(rstd[:, k % 2, :], var_eps[:, k % 2, :], half_neg[:, :],
                                       ALU.pow).then_inc(rstd_ready, 1)
                elif step[0] == "project":
                    g = step[1]
                    cols = slice(g * GROUP, (g + 1) * GROUP)
                    pool.wait_ge(piece_ready[1], g + 1)
                    pool.tensor_tensor(piece[2][:, :, cols], left[:, g % 2], piece[1][:, :, cols],
                                       ALU.subtract).then_inc(piece_ready[2], 1)
                elif step[0] == "scores" and step[2] == HALF - 1 and step[1] in diagonal:
                    b = step[1]
                    q0 = first_query(b)
                    part = probs[:, b % PROB_BUFS, :, q0:q0 + P]
                    pool.wait_ge(act_drained, act_slot[step] + 1)
                    pool.affine_select(out=part, in_=part, compare_op=ALU.is_ge, fill=0.0, base=0,
                                       pattern=[[0, HALF], [1, P]], channel_multiplier=-1).then_inc(masked, 1)

        @block.scalar
        def _(act):
            def drained(instruction):
                instruction.then_inc(act_drained, 1)

            act.wait_ge(mod_in, 32)
            act.activation(silu[:, 0:1], c_col[:, :], ACT.Exp, scale=-1.0).then_inc(exp_c, 1)
            for step in steps:
                if step in act_slot:
                    k = act_slot[step]
                    bank = act_ps[:, k % ACT_RING, :]
                    act.wait_ge(act_filled, k + 1)
                if step[0] == "scores":
                    _, b, e = step
                    q0 = first_query(b)
                    if b >= PROB_BUFS:
                        act.wait_ge(pv_done, b - PROB_BUFS + 1)
                    drained(act.activation(probs[:, b % PROB_BUFS, e, q0:], bank[:, q0:], ACT.Exp, scale=SCORE_SCALE))
                elif step[0] == "weights":
                    drained(act.copy(w_t[:, :, :], bank[:, 0:3 * D].rearrange("p (w n) -> p w n", w=3)))
                elif step[0] == "ffn_weights":
                    act.copy(out_w_t[:, :], bank[:, 0:D])
                    drained(act.copy(gate_w_t[:, :], bank[:, D:D + NE]))
                elif step[0] == "norm_t":
                    g = step[1]
                    act.wait_ge(gates_ready, 1)
                    drained(act.activation(h_t[:, g * GROUP:(g + 1) * GROUP], bank, ACT.Identity,
                                           scale=mod_col[:, 2:3], bias=mod_col[:, 0:1]))
                elif step[0] == "project":
                    g = step[1]
                    act.wait_ge(vec_filled, vec_slot[step] + 1)
                    act.copy(piece[0][:, :, g * GROUP:(g + 1) * GROUP],
                             vec_ps[:, vec_slot[step] % VEC_RING]).then_inc(piece_ready[0], 1)
                elif step[0] == "values":
                    g = step[1]
                    act.wait_ge(const_ready, CONSTS["v_one"])
                    drained(act.copy(v_aug[:, TG * g:TG * g + TG, :, 0:HD],
                                     bank.rearrange("p (t h d) -> p t h d", t=TG, h=NH)))
                elif step[0] == "max_t":
                    n = step[1]
                    if n >= 2:
                        act.wait_ge(max_in[n - 2], 64)
                    rows = bank.bitcast(BF16)[0:8, 0:GROUP]
                    drained(act.copy(max_row[:, n % 2, :], rows))
                elif step[0] == "context":
                    n = step[1]
                    act.wait_ge(pv_done, last_batch[n] + 1)
                    if n >= 2:
                        act.wait_ge(vec_filled, vec_slot[("context_t", n - 2)] + 1)
                    act.copy(ctx_t[:, n % 2, :], ctx_ps[:, :]).then_inc(ctx_copied, 1)
                elif step[0] == "norm2_t":
                    g = step[1]
                    if g:
                        act.wait_ge(vec_filled, vec_slot[("ffn", g - 1)] + 1)
                    drained(act.activation(h2_t[:, :], bank, ACT.Identity,
                                           scale=mod_col[:, 3:4], bias=mod_col[:, 1:2]))
                elif step[0] == "logits":
                    g = step[1]
                    if g:
                        act.wait_ge(shift_ready, g)
                    drained(act.copy(logits[:, :, :], bank[:, 0:TG * NE].rearrange("p (t e) -> p t e", t=TG)))
                elif step[0] == "gate":
                    g = step[1]
                    act.wait_ge(shift_ready, g + 1)
                    act.activation(gate_e[:, :, :], shifted[:, :, :], ACT.Exp).then_inc(gate_exp, 1)

        @block.vector
        def _(dve):
            chain = [0]

            def link(instruction):
                chain[0] += 1
                instruction.then_inc(vec_order, 1)
                dve.wait_ge(vec_order, chain[0])

            dve.wait_ge(exp_c, 1)
            link(dve.tensor_scalar(silu[:, 1:2], silu[:, 0:1], 1.0, None, ALU.add))
            link(dve.reciprocal(silu[:, 2:3], silu[:, 1:2]))
            link(dve.tensor_tensor(silu[:, 3:4], c_col[:, :], silu[:, 2:3], ALU.mult))
            dve.wait_ge(const_ready, CONSTS["ones"])
            dve.tensor_scalar(silu_wide[:, :], ones[:, :], silu[:, 3:4], None, ALU.mult).then_inc(silu_ready, 1)

            for step in steps:
                if step in vec_slot:
                    k = vec_slot[step]
                    banks = vec_ps[:, k % VEC_RING]
                    dve.wait_ge(vec_filled, k + 1)
                if step[0] == "maxima":
                    _, n, i, e, c = step
                    width = min(BANK, (TG * (n // 2) + i + 1) * P - c * BANK)
                    dve.tensor_reduce(part_max[:, n % 2, i, :, e, c], banks[:, :, 0:width], AX.X,
                                      ALU.max).then_inc(vec_drained, 1)
                elif step[0] in ("stats", "stats2"):
                    g, k = step[1], norm_no[step]
                    if step[0] == "stats":
                        dve.wait_ge(x_in_sem[g], 16)
                    for t in range(TG):
                        instruction = dve.bn_stats(bn[:, t, :], x_sb[:, TG * g + t, :])
                    link(instruction)
                    for t in range(TG):
                        instruction = dve.bn_aggr(mean_var[:, k % 2, t, :], bn[:, t, :])
                    link(instruction)
                    if k >= 2:
                        dve.wait_ge(rstd_ready, k - 1)
                    dve.tensor_scalar(var_eps[:, k % 2, :], mean_var[:, k % 2, :, 1], EPS, None,
                                      ALU.add).then_inc(var_ready, 1)
                elif step[0] in ("normalize", "normalize2"):
                    g = step[1]
                    k = norm_no[("stats" + step[0][9:], g)]
                    if k >= 2:
                        name, h = norms[k - 2]
                        dve.wait_ge(act_filled, act_slot[("norm" + name[5:] + "_t", h)] + 1)
                    dve.wait_ge(rstd_ready, k + 1)
                    for t in range(TG):
                        dve.tensor_scalar(normed[:, k % 2, t, :], x_sb[:, TG * g + t, :], mean_var[:, k % 2, t, 0:1],
                                          rstd[:, k % 2, t:t + 1], ALU.subtract, ALU.mult).then_inc(norm_ready, 1)
                elif step[0] == "modulation":
                    dve.tensor_copy(mod_col[:, 0:2], banks[:, 0, 0:2])
                    dve.tensor_scalar(mod_col[:, 2:4], banks[:, 0, 2:4], 1.0, None, ALU.add)
                    raw = banks[:, 1, 0:2 * D].rearrange("p (g d) -> p g d", g=2)
                    dve.tensor_copy(gate_raw[:, :, :], raw).then_inc(vec_drained, 1)
                    dve.wait_ge(vec_drained, k + 1)
                    link(dve.tensor_scalar(gate_sign[:, :, :], gate_raw[:, :, :], 0.0, 2.0, ALU.is_ge, ALU.mult))
                    link(dve.tensor_scalar(gate_sign[:, :, :], gate_sign[:, :, :], -1.0, None, ALU.add))
                    link(dve.scalar_tensor_tensor(gate_size[:, :, :], gate_raw[:, :, :], -1.0, gate_raw[:, :, :],
                                                  ALU.mult, ALU.max))
                    link(dve.scalar_tensor_tensor(gates[:, :, :], gate_size[:, :, :], GATE_FLOOR, gate_sign[:, :, :],
                                                  ALU.max, ALU.mult))
                    dve.wait_ge(act_drained, act_slot[("weights",)] + 1)
                    dve.tensor_tensor(wv_gated[:, :], w_t[:, 2, :], gates[:, 0, :],
                                      ALU.mult).then_inc(gates_ready, 1)
                elif step[0] == "expert_out":
                    dve.tensor_tensor(ffn_w[:, :, :], banks[:, 0, 0:2 * D].rearrange("p (e d) -> p e d", e=2),
                                      gates[:, 1:2, :].broadcast_to([P, 2, D]), ALU.mult).then_inc(vec_drained, 1)
                elif step[0] == "project":
                    g = step[1]
                    cols = slice(g * GROUP, (g + 1) * GROUP)
                    dve.wait_ge(piece_ready[0], g + 1)
                    if g >= 2:
                        dve.wait_ge(piece_ready[2], g - 1)
                    dve.tensor_tensor(left[:, g % 2], banks, piece[0][:, :, cols],
                                      ALU.subtract).then_inc(vec_drained, 1)
                    dve.wait_ge(vec_drained, k + 1)
                    dve.tensor_copy(piece[1][:, :, cols], left[:, g % 2]).then_inc(piece_ready[1], 1)
                elif step[0] == "max_sum":
                    n = step[1]
                    g = n // 2
                    dve.wait_ge(vec_drained, vec_slot[("maxima", n, TG - 1, HALF // 2 - 1, g)] + 1)
                    link(dve.tensor_reduce(neg_max[:, :], part_max[:, n % 2, :, :, :, 0:g + 1].rearrange(
                        "p i t e c -> p (i t e) c"), AX.X, ALU.max, negate=True))
                    whole = neg_max[:, :].rearrange("p (i e) -> p i e", e=2)
                    pieces = max_piece[:, n % 2].rearrange("p i t a e -> p (i t) a e")
                    if n >= 2:
                        dve.wait_ge(act_filled, act_slot[("max_t", n - 2)] + 1)
                    link(dve.tensor_copy(pieces[:, :, 0, :], whole))
                    dve.tensor_tensor(pieces[:, :, 1, :], whole, pieces[:, :, 0, :],
                                      ALU.subtract).then_inc(max_ready, 1)
                    dve.wait_ge(max_ready, n + 1)
                elif step[0] == "context_t":
                    n = step[1]
                    g, first = n // 2, (n % 2) * HALF * HD
                    heads = banks[:, 0, :].rearrange("p (t h v) -> p t h v", t=TG, h=HALF)
                    link(dve.reciprocal(sum_inv[:, :, :], heads[:, :, :, HD]))
                    dve.tensor_tensor(ctx_norm[:, :, :].rearrange("p t (h d) -> p t h d", h=HALF),
                                      heads[:, :, :, 0:HD],
                                      sum_inv[:, :, :].unsqueeze(3).broadcast_to([P, TG, HALF, HD]),
                                      ALU.mult).then_inc(vec_drained, 1)
                    dve.wait_ge(vec_drained, k + 1)
                    part = x_sb[:, TG * g:TG * g + TG, first:first + HALF * HD]
                    link(dve.tensor_tensor(part, part, ctx_norm[:, :, :], ALU.add))
                elif step[0] == "gate":
                    g = step[1]
                    dve.wait_ge(act_drained, act_slot[("logits", g)] + 1)
                    link(dve.tensor_reduce(top[:, :], logits[:, :, :], AX.X, ALU.max))
                    dve.tensor_tensor(shifted[:, :, :], logits[:, :, :],
                                      top[:, :].unsqueeze(2).broadcast_to([P, TG, NE]),
                                      ALU.subtract).then_inc(shift_ready, 1)
                    dve.wait_ge(gate_exp, g + 1)
                    link(dve.tensor_reduce(gate_sum[:, :], gate_e[:, :, :], AX.X, ALU.add))
                    link(dve.reciprocal(gate_inv[:, :], gate_sum[:, :]))
                    link(dve.tensor_tensor(gate_p[:, :, :], gate_e[:, :, :],
                                           gate_inv[:, :].unsqueeze(2).broadcast_to([P, TG, NE]), ALU.mult))
                    link(dve.tensor_scalar(flags[:, :, :], gate_p[:, :, :], TOP_P, None, ALU.is_gt))
                    link(dve.tensor_reduce(count[:, :, 1], flags[:, :, :], AX.X, ALU.add))
                    link(dve.tensor_scalar(count[:, :, 0], count[:, :, 1], -1.0, float(NE), ALU.mult, ALU.add))
                    link(dve.tensor_tensor(expert_scale[:, :, :], count[:, :, :], gate_p[:, :, 0:2], ALU.mult))
                elif step[0] == "ffn":
                    g = step[1]
                    if g >= 2:
                        dve.wait_ge(out_stored[g - 2], 16)
                    flat = banks.rearrange("p b (t e d) -> p (b t) e d", t=TG // 2, e=2)
                    for t in range(TG):
                        instruction = dve.scalar_tensor_tensor(
                            ffn_part[:, t, :], flat[:, t, 0, :], expert_scale[:, t, 0:1], x_sb[:, TG * g + t, :],
                            ALU.mult, ALU.add)
                    link(instruction)
                    for t in range(TG):
                        instruction = dve.scalar_tensor_tensor(
                            result[:, g % 2, t, :], flat[:, t, 1, :], expert_scale[:, t, 1:2], ffn_part[:, t, :],
                            ALU.mult, ALU.add)
                        if t == TG - 2:
                            instruction.then_inc(vec_order, 1)
                            chain[0] += 1
                            dve.wait_ge(vec_order, chain[0])
                    instruction.then_inc(vec_drained, 1)

        @block.tensor
        def _(pe):
            for step in steps:
                if step in act_slot:
                    k = act_slot[step]
                    bank = act_ps[:, k % ACT_RING, :]
                    filled = act_filled
                    if k >= ACT_RING:
                        pe.wait_ge(act_drained, k - ACT_RING + 1)
                if step in vec_slot:
                    k = vec_slot[step]
                    banks = vec_ps[:, k % VEC_RING]
                    filled = vec_filled
                    if k >= VEC_RING:
                        pe.wait_ge(vec_drained, k - VEC_RING + 1)
                last = None
                if step[0] == "scores":
                    _, b, e = step
                    n, j = batches[b]
                    g, h, q0 = n // 2, HALF * (n % 2) + e, first_query(b)
                    if j == 0 and e == 0:
                        pe.wait_ge(max_in[n], 64)
                        if n == 0:
                            pe.wait_ge(ones_in, 16 * NH)
                        pe.wait_ge(rest_in[g], 16 * N_REST)
                    rows = stack_rows[h % 2]
                    last = pe.matmul(bank[:, q0:], k_stack[0:rows, h, j * P:(j + 1) * P],
                                     q_stack[0:rows, h, g * GROUP + q0:(g + 1) * GROUP], start=True, stop=True)
                elif step[0] == "maxima":
                    _, n, i, e, c = step
                    g = n // 2
                    tile = TG * g + i
                    pe.wait_ge(main_in[g], 16 * N_MAIN)
                    width = min(BANK, (tile + 1) * P - c * BANK)
                    for odd in range(2):
                        h = HALF * (n % 2) + 2 * e + odd
                        r = main_at[odd]
                        last = pe.matmul(banks[:, odd, 0:width], q_stack[r:r + MAIN, h, tile * P:(tile + 1) * P],
                                         k_stack[r:r + MAIN, h, c * BANK:c * BANK + width],
                                         start=True, stop=c < g)
                    if c == g:
                        pe.wait_ge(const_ready, CONSTS["mask"])
                        for odd in range(2):
                            last = pe.matmul(banks[:, odd, width - P:width], ident_bf[:, :], mask[:, :],
                                             start=False, stop=True)
                elif step[0] == "probs_v":
                    b = step[1]
                    n, j = batches[b]
                    g, q0 = n // 2, first_query(b)
                    pe.wait_ge(act_drained, act_slot[("scores", b, HALF - 1)] + 1)
                    if b in diagonal:
                        pe.wait_ge(masked, masks_until(b))
                    if j % TG == 0 and n % 2 == 0 and j // TG == g:
                        pe.wait_ge(act_drained, act_slot[("values", g)] + 1)
                    if j == 0 and n:
                        pe.wait_ge(ctx_copied, n)
                    for e in range(HALF):
                        last = pe.matmul(ctx_ps[VW * e:VW * e + VW, q0:], v_aug[:, j, HALF * (n % 2) + e, :],
                                         probs[:, b % PROB_BUFS, e, q0:], start=(j == 0),
                                         stop=(j == TG * g + TG - 1))
                    filled = pv_done
                elif step[0] == "weights":
                    pe.wait_ge(const_ready, CONSTS["ident"])
                    pe.wait_ge(w_in, 16 * 5)
                    for w in range(3):
                        last = pe.transpose(bank[:, w * D:(w + 1) * D], w_sb[:, w, :], ident[:, :])
                elif step[0] == "ffn_weights":
                    pe.transpose(bank[:, 0:D], w_sb[:, 3, :], ident[:, :])
                    last = pe.transpose(bank[:, D:D + NE], gate_w[:, :], ident[0:NE, 0:NE])
                elif step[0] == "modulation":
                    pe.wait_ge(silu_ready, 1)
                    for m, s in enumerate((0, 3, 1, 4)):
                        pe.matmul(banks[:, 0, m:m + 1], wmod[:, s, :], silu[:, 3:4], start=True, stop=True)
                    for m, s in enumerate((2, 5)):
                        last = pe.matmul(banks[:, 1, m * D:(m + 1) * D], silu_wide[:, :], wmod[:, s, :],
                                         start=True, stop=True)
                elif step[0] == "expert_out":
                    pe.wait_ge(expert_in, 16)
                    pe.wait_ge(act_drained, act_slot[("ffn_weights",)] + 1)
                    for m in range(2):
                        last = pe.matmul(banks[:, 0, m * D:(m + 1) * D], expert_w[:, m, :], out_w_t[:, :],
                                         start=True, stop=True)
                elif step[0] in ("norm_t", "norm2_t"):
                    m = norm_no[("stats" + step[0][4:-2], step[1])]
                    for t in range(TG):
                        pe.wait_ge(norm_ready, TG * m + t + 1)
                        last = pe.transpose(bank[:, t * P:(t + 1) * P], normed[:, m % 2, t, :], ident[:, :])
                elif step[0] == "project":
                    g = step[1]
                    pe.wait_ge(act_drained, act_slot[("norm_t", g)] + 1)
                    for qk in range(2):
                        last = pe.matmul(banks[:, qk, :], w_t[:, qk, :], h_t[:, g * GROUP:(g + 1) * GROUP],
                                         start=True, stop=True)
                elif step[0] == "values":
                    g = step[1]
                    pe.wait_ge(gates_ready, 1)
                    for t in range(TG):
                        last = pe.matmul(bank[:, t * D:(t + 1) * D], h_t[:, (TG * g + t) * P:(TG * g + t + 1) * P],
                                         wv_gated[:, :], start=True, stop=True)
                elif step[0] == "max_t":
                    n = step[1]
                    pe.wait_ge(max_ready, n + 1)
                    rows = bank.bitcast(BF16)
                    for i in range(TG):
                        last = pe.transpose(rows[0:8, i * P:(i + 1) * P],
                                            max_piece[:, n % 2, i].rearrange("p t a e -> p (t a e)"), ident_bf[:, :])
                elif step[0] == "context_t":
                    n = step[1]
                    pe.wait_ge(ctx_copied, n + 1)
                    for t in range(TG):
                        last = pe.transpose(banks[:, 0, t * P:(t + 1) * P], ctx_t[:, n % 2, t * P:(t + 1) * P],
                                            ident[:, :])
                elif step[0] == "logits":
                    g = step[1]
                    pe.wait_ge(act_drained, act_slot[("norm2_t", g)] + 1)
                    for t in range(TG):
                        last = pe.matmul(bank[:, t * NE:(t + 1) * NE], h2_t[:, t * P:(t + 1) * P], gate_w_t[:, :],
                                         start=True, stop=True)
                elif step[0] == "ffn":
                    g = step[1]
                    for t in range(TG):
                        last = pe.matmul(banks[:, t // 2, (t % 2) * 2 * D:(t % 2 + 1) * 2 * D],
                                         h2_t[:, t * P:(t + 1) * P], ffn_w[:, :, :].rearrange("p e d -> p (e d)"),
                                         start=True, stop=True)
                if last is not None:
                    last.then_inc(filled, 1)


_INS = ["L0_attn_hidden_states", "L0_attn_Wq", "L0_attn_Wk", "L0_attn_Wv", "L0_ffn_gate_W", "L0_ffn_expert_W",
        "L0_ffn_out_W", "L0_c", "L0_wmod"]


def kernel(**inputs):
    import numpy as np
    import concourse.bacc as bacc
    from concourse.bass_utils import run_bass_kernel_spmd

    nc = bacc.Bacc("TRN2", target_bir_lowering=False, num_devices=1)
    arrays, args = {}, []
    for name in _INS:
        a = np.ascontiguousarray(inputs[name])
        arrays[f"in_{name}"] = a
        args.append(nc.dram_tensor(f"in_{name}", a.shape, mybir.dt.from_np(a.dtype), kind="ExternalInput").ap())
    out = nc.dram_tensor("out_x", (1, S, D), F32, kind="ExternalOutput").ap()
    block_kernel(nc, *args, out)
    r = run_bass_kernel_spmd(nc, [arrays], core_ids=[0])
    return r.results[0]["out_x"]
```

```python
from contextlib import ExitStack

import concourse.bass as bass
from concourse import mybir

F32 = mybir.dt.float32
BF16 = mybir.dt.bfloat16
ALU = mybir.AluOpType
ACT = mybir.ActivationFunctionType
AX = mybir.AxisListType

P = 128
S, D = 2048, 128
NH = 8
HD = D // NH
NE = 8
TOP_P = 0.3
EPS = 1e-5
GATE_FLOOR = 0.25
NT = S // P
TG = 4
GROUP = TG * P
NG = S // GROUP
HALF = 4
NI = 2 * NG
VW = 32
PRODUCTS = [(0, 0), (0, 1), (0, 2), (1, 0), (1, 1), (1, 2), (2, 0)]
NPR = len(PRODUCTS)
ROWS = NPR * HD
SHIFT_ROWS = 2
SCORE_SCALE = HD ** -0.5
MASKED = -(2.0 ** 100)
ACT_RING, VEC_RING = 3, 2
PROB_BUFS = 4
PREPARED_AFTER = {2: 0, 3: 2}
BANK = 512

IN_ACT_RING = {"spread", "weights", "ffn_weights", "norm_t", "values", "max_t", "scores", "norm2_t", "logits"}
IN_VEC_RING = {"modulation", "expert_out", "project", "maxima", "context_t", "ffn"}


def item_batches():
    return [(n, j) for n in range(NI) for j in range(TG * (n // 2) + TG)]


def score_width(n, j):
    return GROUP - max(0, j - TG * (n // 2)) * P


def maxima_width(n, i, c):
    return min(BANK, (TG * (n // 2) + i + 1) * P - c * BANK)


def prepare(g):
    return [("stats", g), ("normalize", g), ("norm_t", g), ("project", g), ("middle", g), ("values", g)]


def plan():
    batches = item_batches()
    maxima = [[("maxima", n, i, e, c) for i in range(TG) for e in range(HALF // 2) for c in range(n // 2 + 1)]
              for n in range(NI)]
    order = [("warm", 16), ("stats", 0), ("silu",), ("spread_rows",), ("weights",), ("ffn_weights",),
             ("modulation",), ("stats", 1), ("normalize", 0), ("warm", 3), ("norm_t", 0), ("warm", 4),
             ("project", 0), ("normalize", 1), ("constants",), ("middle", 0), ("norm_t", 1), ("warm", 4),
             ("gates",)]
    spreads = [("spread", h, qk) for h in range(NH) for qk in (1, 0)]
    order += spreads[0:4] + [("project", 1), ("middle", 1)]
    for k, m in enumerate([m for e in range(2) for m in maxima[0] if m[3] == e]):
        order += [m] + (spreads[4 + k:5 + k] if k < 4 else spreads[2 * k:2 * k + 2])
    order += [("max_sum", 0), ("values", 0), ("max_t", 0), ("expert_out",), ("values", 1)]

    def cost(s):
        if s[0] == "scores":
            w = score_width(*batches[s[1]])
            return w / 2.4 + 3, w / 1.2 + 51, 200
        if s[0] == "maxima":
            w = maxima_width(s[1], s[2], s[4])
            return w / 1.2 + 6 + (110 if s[4] == s[1] // 2 else 0), 2 * w * 1.042 + 65, 200
        if s[0] == "probs_v":
            return score_width(*batches[s[1]]) * 4 / 2.4 + 80, 0, 200
        return {"context": (0, 480, 200), "context_t": (430, 850, 200), "stats2": (0, 1700, 2300),
                "normalize2": (0, 1600, 200), "middle": (0, 904, 20000), "gate_shift": (0, 300, 700), "norm2_t": (430, 620, 200), "logits": (430, 230, 200),
                "gate": (0, 800, 200), "ffn": (1720, 1700, 200), "max_sum": (0, 350, 200),
                "max_t": (220, 480, 2600), "stats": (0, 1700, 2300), "normalize": (0, 1600, 200),
                "norm_t": (430, 620, 200), "project": (1710, 2400, 200), "values": (860, 480, 200)}[s[0]]

    on_act = {"scores", "middle", "context", "norm2_t", "logits", "max_t", "norm_t", "values", "normalize", "normalize2"}
    maxima_stream = []
    for n in range(1, NI):
        maxima_stream += maxima[n] + [("max_sum", n), ("max_t", n)]
    streams = [[], prepare(2) + prepare(3), maxima_stream, [("probs_v", b) for b in range(len(batches))],
               [("scores", b, e) for b in range(len(batches)) for e in range(HALF)]]
    done = {s: 0.0 for s in order}
    done[("max_t", 0)] = 3000.0
    last_batch = {n: b for b, (n, _) in enumerate(batches)}
    now = {"pe": 0.0, "act": 0.0, "vec": 0.0}
    drained = {"act": [0.0] * ACT_RING, "vec": [0.0] * VEC_RING}

    def ready(s):
        if s[0] == "scores":
            needs = [("max_t", batches[s[1]][0])] + ([("probs_v", s[1] - PROB_BUFS)] if s[1] >= PROB_BUFS else [])
        elif s[0] == "probs_v":
            n, j = batches[s[1]]
            needs = [("scores", s[1], HALF - 1)] + ([("context", n - 1)] if n and j == 0 else [])
        elif s[0] == "maxima":
            needs = [("middle", s[1] // 2)]
        else:
            needs = [before[s]] if s in before else []
        if any(m not in done for m in needs):
            return None
        late = 700 if s[0] == "probs_v" and j >= TG * (n // 2) else 0
        return max([done[m] for m in needs] + [0.0]) + late

    before = {("stats", g): ("max_sum", n) for g, n in PREPARED_AFTER.items()}
    for n in range(NI):
        before[("max_sum", n)] = maxima[n][-1]
        before[("max_t", n)] = ("max_sum", n)
        before[("context", n)] = ("probs_v", last_batch[n])
        before[("context_t", n)] = ("context", n)
    for g in range(NG):
        for chain in ([("context_t", 2 * g + 1), ("stats2", g), ("normalize2", g), ("norm2_t", g), ("logits", g),
                       ("gate_shift", g), ("gate", g), ("ffn", g)], prepare(g)):
            before |= dict(zip(chain[1:], chain[:-1]))
        before[("values", g)] = ("norm_t", g)
    while any(streams):
        options = []
        for rank, stream in enumerate(streams):
            if stream and (at := ready(stream[0])) is not None:
                s = stream[0]
                ring = "act" if s[0] in IN_ACT_RING else "vec" if s[0] in IN_VEC_RING else None
                if ring:
                    at = max(at, drained[ring][0])
                options.append((max(at, now["pe"]), rank))
        start, rank = min(options)
        s = streams[rank].pop(0)
        on_pe, taken, passes = cost(s)
        if on_pe:
            now["pe"] = start + on_pe
        end = start + on_pe
        if taken:
            engine = "act" if s[0] in on_act else "vec"
            now[engine] = end = max(now[engine], end + 100) + taken
        if s[0] in IN_ACT_RING:
            drained["act"] = drained["act"][1:] + [end + 60]
        if s[0] in IN_VEC_RING:
            drained["vec"] = drained["vec"][1:] + [end + 60]
        done[s] = end + passes
        order.append(s)
        if s[0] == "probs_v" and last_batch[batches[s[1]][0]] == s[1]:
            n = batches[s[1]][0]
            streams[0] += [("context", n), ("context_t", n)]
            if n % 2:
                streams[0] += [("stats2", n // 2), ("normalize2", n // 2), ("norm2_t", n // 2), ("logits", n // 2),
                               ("gate_shift", n // 2), ("gate", n // 2), ("ffn", n // 2)]
    return order


def block_kernel(nc, x_in, wq_in, wk_in, wv_in, gate_w_in, expert_w_in, out_w_in, c_in, wmod_in, out):
    steps = plan()
    batches = item_batches()
    last_batch = {n: b for b, (n, _) in enumerate(batches)}
    act_slot = {s: k for k, s in enumerate([s for s in steps if s[0] in IN_ACT_RING])}
    vec_slot = {s: k for k, s in enumerate([s for s in steps if s[0] in IN_VEC_RING])}
    diagonal = [b for b, (n, j) in enumerate(batches) if j >= TG * (n // 2)]

    def first_query(b):
        n, j = batches[b]
        return max(0, j - TG * (n // 2)) * P

    def masks_until(b):
        return sum(1 for d in diagonal if d <= b)

    with ExitStack() as ctx:
        def sb(name, shape, dt):
            return ctx.enter_context(nc.sbuf_tensor(name, shape, dt))

        def sem(name):
            return ctx.enter_context(nc.semaphore(name))

        act_ps = ctx.enter_context(nc.psum_tensor("act_ps", [P, ACT_RING, BANK], F32))
        vec_ps = ctx.enter_context(nc.psum_tensor("vec_ps", [P, VEC_RING, 2, BANK], F32))
        ctx_ps = ctx.enter_context(nc.psum_tensor("ctx_ps", [P, BANK], F32))

        x_sb = sb("x_sb", [P, NT, D], F32)
        w_sb = sb("w_sb", [P, 4, D], F32)
        w_t = sb("w_t", [P, 3, D], F32)
        wv_gated = sb("wv_gated", [P, D], F32)
        out_w_t = sb("out_w_t", [P, D], F32)
        gate_w = sb("gate_w", [NE, D], F32)
        gate_w_t = sb("gate_w_t", [P, NE], F32)
        expert_w = sb("expert_w", [P, 2, D], F32)
        ffn_w = sb("ffn_w", [P, 2, D], F32)
        c_col = sb("c_col", [P, 1], F32)
        silu = sb("silu", [P, 4], F32)
        silu_wide = sb("silu_wide", [P, P], F32)
        wmod = sb("wmod", [P, 6, D], F32)
        mod_col = sb("mod_col", [P, 4], F32)
        gates = sb("gates", [P, 2, D], F32)
        gate_raw = sb("gate_raw", [P, 2, D], F32)
        gate_sign = sb("gate_sign", [P, 2, D], F32)
        gate_size = sb("gate_size", [P, 2, D], F32)
        ident = sb("ident", [P, P], F32)
        ident_bf = sb("ident_bf", [P, P], BF16)
        mask = sb("mask", [P, P], BF16)
        ones = sb("ones", [P, P], F32)
        ones_row = sb("ones_row", [2, S], BF16)
        zeros = sb("zeros", [P, BANK], BF16)
        half_neg = sb("half_neg", [P, TG], F32)
        bn = sb("bn", [P, TG, 6], F32)
        mean_var = sb("mean_var", [P, 2, TG, 2], F32)
        var_eps = sb("var_eps", [P, 2, TG], F32)
        rstd = sb("rstd", [P, 2, TG], F32)
        norm_shift = sb("norm_shift", [P, 2, TG], F32)
        normed = sb("normed", [P, 2, TG, D], F32)
        h_t = sb("h_t", [P, S], F32)
        piece = [sb(f"piece{k}", [P, 2, S], BF16) for k in range(3)]
        left = sb("left", [P, 2, GROUP], F32)
        q_stack = sb("q_stack", [P, NH, S], BF16)
        k_stack = sb("k_stack", [P, NH, S], BF16)
        v_aug = sb("v_aug", [P, NT, NH, VW], F32)
        part_max = sb("part_max", [P, 2, TG, HALF, NG], F32)
        neg_max = sb("neg_max", [P, TG * HALF], F32)
        max_piece = sb("max_piece", [P, 2, TG, SHIFT_ROWS, HALF], BF16)
        max_row = sb("max_row", [SHIFT_ROWS * HALF, 2, GROUP], BF16)
        spread = sb("spread", [P, 2, 3, NH, NPR, HD], BF16)
        probs = sb("probs", [P, PROB_BUFS, HALF, GROUP], F32)
        ctx_t = sb("ctx_t", [P, 2, GROUP], F32)
        ctx_norm = sb("ctx_norm", [P, TG, HALF * HD], F32)
        sum_inv = sb("sum_inv", [P, TG, HALF], F32)
        h2_t = sb("h2_t", [P, GROUP], F32)
        logits = sb("logits", [P, TG, NE], F32)
        top = sb("top", [P, TG], F32)
        shifted = sb("shifted", [P, TG, NE], F32)
        gate_e = sb("gate_e", [P, TG, NE], F32)
        gate_sum = sb("gate_sum", [P, TG], F32)
        gate_inv = sb("gate_inv", [P, TG], F32)
        gate_p = sb("gate_p", [P, TG, NE], F32)
        flags = sb("flags", [P, TG, NE], F32)
        count = sb("count", [P, TG, 2], F32)
        expert_scale = sb("expert_scale", [P, TG, 2], F32)
        result = sb("result", [P, 2, TG, D], F32)

        scratch = nc.dram_tensor("piece_scratch", (3, 2, D, S), BF16, kind="Internal").ap()

        x_in_sem = [sem(f"x_in{g}") for g in range(NG)]
        w_in = sem("w_in")
        c_loaded = sem("c_loaded")
        mod_in = sem("mod_in")
        expert_in = sem("expert_in")
        const_ready = sem("const_ready")
        ones_in = sem("ones_in")
        act_filled = sem("act_filled")
        act_drained = sem("act_drained")
        vec_filled = sem("vec_filled")
        vec_drained = sem("vec_drained")
        vec_order = sem("vec_order")
        zeros_ready = sem("zeros_ready")
        exp_c = sem("exp_c")
        silu_ready = sem("silu_ready")
        gates_ready = sem("gates_ready")
        wv_ready = sem("wv_ready")
        var_ready = sem("var_ready")
        rstd_ready = sem("rstd_ready")
        pool_order = sem("pool_order")
        norm_ready = sem("norm_ready")
        piece_ready = [sem(f"piece_ready{k}") for k in range(3)]
        stored = [sem(f"stored{g}") for g in range(NG)]
        stored_lo = [sem(f"stored_lo{g}") for g in range(NG)]
        stack_in = [sem(f"stack_in{g}") for g in range(NG)]
        max_ready = sem("max_ready")
        max_in = [sem(f"max_in{n}") for n in range(NI)]
        masked = sem("masked")
        pv_done = sem("pv_done")
        ctx_copied = sem("ctx_copied")
        shift_ready = sem("shift_ready")
        gate_exp = sem("gate_exp")
        out_stored = [sem(f"out_stored{g}") for g in range(NG)]

        CONSTS = dict(ident=2, ones=3, half_neg=4, spread=5 + 2 * NPR, ident_bf=7 + 2 * NPR, mask=9 + 2 * NPR, ones_row=10 + 2 * NPR, v_one=12 + 2 * NPR)
        norms = [s for s in steps if s[0] in ("stats", "stats2")]
        norm_no = {s: k for k, s in enumerate(norms)}

        x_tiles = x_in.rearrange("b (t p) d -> p (b t) d", p=P)
        out_tiles = out.rearrange("b (t p) d -> p (b t) d", p=P)

        block = ctx.enter_context(nc.Block())

        @block.sync
        def _(sp):
            for g in range(NG):
                sp.dma_start(x_sb[:, TG * g:TG * g + TG, :],
                             x_tiles[:, TG * g:TG * g + TG, :]).then_inc(x_in_sem[g], 16)
            sp.wait_ge(const_ready, CONSTS["ones_row"])
            sp.dma_start(k_stack[ROWS:ROWS + SHIFT_ROWS, :, :],
                         ones_row[:, :].unsqueeze(1).broadcast_to([SHIFT_ROWS, NH, S])).then_inc(ones_in, 16)

            for step in steps:
                if step[0] == "project" and step[1]:
                    g = step[1]
                    cols = slice(g * GROUP, (g + 1) * GROUP)
                    for k in range(3):
                        sp.wait_ge(piece_ready[k], g + 1)
                        sp.dma_start(scratch[k, :, :, cols].rearrange("a p c -> p a c"),
                                     piece[k][:, :, cols]).then_inc(stored[g] if k < 2 else stored_lo[g], 16)
                    sp.wait_ge(stored[g], 32)
                    lowest = [(r, qk) for r, pair in enumerate(PRODUCTS) for qk in range(2) if pair[qk] == 2]
                    higher = [(r, qk) for r, pair in enumerate(PRODUCTS) for qk in range(2) if pair[qk] != 2]
                    for r, qk in higher + lowest:
                        if (r, qk) == lowest[0]:
                            sp.wait_ge(stored_lo[g], 16)
                        src = scratch[PRODUCTS[r][qk], qk, :, cols].rearrange("(h p) c -> p h c", p=HD)
                        sp.dma_start((q_stack, k_stack)[qk][r * HD:(r + 1) * HD, :, cols],
                                     src).then_inc(stack_in[g], 16)
                elif step[0] == "ffn":
                    g = step[1]
                    sp.wait_ge(vec_drained, vec_slot[step] + 1)
                    sp.dma_start(out_tiles[:, TG * g:TG * g + TG, :], result[:, g % 2]).then_inc(out_stored[g], 16)
            for g in range(NG):
                sp.wait_ge(out_stored[g], 16)

        @block.gpsimd
        def _(pool):
            pool.memset(ident[:, :], 0.0).then_inc(const_ready, 1)
            pool.wait_ge(const_ready, 1)
            pool.affine_select(out=ident[:, :], in_=ident[:, :], compare_op=ALU.not_equal, fill=1.0, base=0,
                               pattern=[[-1, P]], channel_multiplier=1).then_inc(const_ready, 1)
            pool.memset(ones[:, :], 1.0).then_inc(const_ready, 1)
            pool.memset(half_neg[:, :], -0.5).then_inc(const_ready, 1)

            for step in steps:
                if step[0] in ("stats", "stats2"):
                    k = norm_no[step]
                    if k == 0:
                        pool.wait_ge(const_ready, CONSTS["half_neg"])
                    pool.wait_ge(var_ready, k + 1)
                    if k >= 2:
                        pool.wait_ge(norm_ready, TG * (k - 1))
                    pool.tensor_tensor(rstd[:, k % 2, :], var_eps[:, k % 2, :], half_neg[:, :],
                                       ALU.pow).then_inc(pool_order, 1)
                    pool.wait_ge(pool_order, 2 * k + 1)
                    pool.tensor_tensor(norm_shift[:, k % 2, :], mean_var[:, k % 2, :, 0], rstd[:, k % 2, :],
                                       ALU.mult).then_inc(pool_order, 1)
                    pool.wait_ge(pool_order, 2 * k + 2)
                    pool.tensor_scalar(norm_shift[:, k % 2, :], norm_shift[:, k % 2, :], -1.0, None,
                                       ALU.mult).then_inc(rstd_ready, 1)
                elif step[0] == "spread_rows":
                    pool.memset(spread[:, :, :, :, :, :].rearrange("p a k h r d -> p (a k h r d)").bitcast(F32),
                                0.0).then_inc(const_ready, 1)
                    pool.wait_ge(const_ready, CONSTS["half_neg"] + 1)
                    for r, pair in enumerate(PRODUCTS):
                        for qk, k in enumerate(pair):
                            part = spread[:, qk, k, :, r, :]
                            pool.affine_select(out=part, in_=part, compare_op=ALU.not_equal, fill=1.0, base=0,
                                               pattern=[[-HD, NH], [-1, HD]],
                                               channel_multiplier=1).then_inc(const_ready, 1)
                elif step[0] == "constants":
                    pool.memset(ident_bf[:, :], 0.0).then_inc(const_ready, 1)
                    pool.wait_ge(const_ready, CONSTS["ident_bf"] - 1)
                    pool.affine_select(out=ident_bf[:, :], in_=ident_bf[:, :], compare_op=ALU.not_equal, fill=1.0,
                                       base=0, pattern=[[-1, P]], channel_multiplier=1).then_inc(const_ready, 1)
                    pool.memset(mask[:, :], 0.0).then_inc(const_ready, 1)
                    pool.wait_ge(const_ready, CONSTS["mask"] - 1)
                    pool.affine_select(out=mask[:, :], in_=mask[:, :], compare_op=ALU.is_ge, fill=MASKED, base=0,
                                       pattern=[[-1, P]], channel_multiplier=1).then_inc(const_ready, 1)
                    pool.memset(ones_row[:, :], 1.0).then_inc(const_ready, 1)
                    pool.memset(v_aug[:, :, :, :], 0.0).then_inc(const_ready, 1)
                    pool.wait_ge(const_ready, CONSTS["v_one"] - 1)
                    pool.memset(v_aug[:, :, :, HD:HD + 1], 1.0).then_inc(const_ready, 1)
                elif step[0] == "middle" and step[1]:
                    g = step[1]
                    cols = slice(g * GROUP, (g + 1) * GROUP)
                    pool.wait_ge(piece_ready[1], g + 1)
                    pool.tensor_tensor(piece[2][:, :, cols], left[:, :, :], piece[1][:, :, cols],
                                       ALU.subtract).then_inc(piece_ready[2], 1)
                elif step[0] == "scores" and step[2] == HALF - 1 and step[1] in diagonal:
                    b = step[1]
                    q0 = first_query(b)
                    part = probs[:, b % PROB_BUFS, :, q0:q0 + P]
                    pool.wait_ge(act_drained, act_slot[step] + 1)
                    pool.affine_select(out=part, in_=part, compare_op=ALU.is_ge, fill=0.0, base=0,
                                       pattern=[[0, HALF], [1, P]], channel_multiplier=-1).then_inc(masked, 1)

        @block.scalar
        def _(act):
            def drained(instruction):
                instruction.then_inc(act_drained, 1)

            act.dma_start(c_col[:, :], c_in.rearrange("a d -> d a")).then_inc(c_loaded, 16)
            act.dma_start(wmod[:, :, :], wmod_in.rearrange("d (s n) -> d s n", s=6)).then_inc(mod_in, 16)
            for k, w in enumerate((wq_in, wk_in, wv_in, out_w_in)):
                act.dma_start(w_sb[:, k, :], w).then_inc(w_in, 16)
            act.dma_start(gate_w[:, :], gate_w_in).then_inc(w_in, 16)
            act.dma_start(expert_w[:, :, :], expert_w_in[0:2].rearrange("e h d -> h e d")).then_inc(expert_in, 16)
            act.wait_ge(c_loaded, 16)
            act.activation(silu[:, 0:1], c_col[:, :], ACT.Exp, scale=-1.0).then_inc(exp_c, 1)
            for step in steps:
                if step in act_slot:
                    k = act_slot[step]
                    bank = act_ps[:, k % ACT_RING, :]
                    act.wait_ge(act_filled, k + 1)
                if step[0] == "scores":
                    _, b, e = step
                    q0 = first_query(b)
                    if b >= PROB_BUFS:
                        act.wait_ge(pv_done, b - PROB_BUFS + 1)
                    drained(act.activation(probs[:, b % PROB_BUFS, e, q0:], bank[:, q0:], ACT.Exp, scale=SCORE_SCALE))
                elif step[0] == "spread":
                    _, h, qk = step
                    drained(act.copy((q_stack, k_stack)[qk][0:ROWS, h, 0:GROUP], bank[0:ROWS, :]))
                elif step[0] == "weights":
                    drained(act.copy(w_t[:, :, :], bank[:, 0:3 * D].rearrange("p (w n) -> p w n", w=3)))
                elif step[0] == "ffn_weights":
                    act.copy(out_w_t[:, :], bank[:, 0:D])
                    drained(act.copy(gate_w_t[:, :], bank[:, D:D + NE]))
                elif step[0] in ("normalize", "normalize2"):
                    g = step[1]
                    k = norm_no[("stats" + step[0][9:], g)]
                    if k >= 2:
                        name, h = norms[k - 2]
                        act.wait_ge(act_filled, act_slot[("norm" + name[5:] + "_t", h)] + 1)
                    act.wait_ge(rstd_ready, k + 1)
                    for t in range(TG):
                        act.activation(normed[:, k % 2, t, :], x_sb[:, TG * g + t, :], ACT.Identity,
                                       scale=rstd[:, k % 2, t:t + 1],
                                       bias=norm_shift[:, k % 2, t:t + 1]).then_inc(norm_ready, 1)
                elif step[0] == "middle" and step[1]:
                    g = step[1]
                    act.wait_ge(vec_drained, vec_slot[("project", g)] + 1)
                    act.copy(piece[1][:, :, g * GROUP:(g + 1) * GROUP], left[:, :, :]).then_inc(piece_ready[1], 1)
                elif step[0] == "norm_t":
                    g = step[1]
                    act.wait_ge(vec_drained, vec_slot[("modulation",)] + 1)
                    drained(act.activation(h_t[:, g * GROUP:(g + 1) * GROUP], bank, ACT.Identity,
                                           scale=mod_col[:, 2:3], bias=mod_col[:, 0:1]))
                elif step[0] == "project":
                    g = step[1]
                    act.wait_ge(vec_filled, vec_slot[step] + 1)
                    act.copy(piece[0][:, :, g * GROUP:(g + 1) * GROUP],
                             vec_ps[:, vec_slot[step] % VEC_RING]).then_inc(piece_ready[0], 1)
                elif step[0] == "values":
                    g = step[1]
                    act.wait_ge(const_ready, CONSTS["v_one"])
                    drained(act.copy(v_aug[:, TG * g:TG * g + TG, :, 0:HD],
                                     bank.rearrange("p (t h d) -> p t h d", t=TG, h=NH)))
                elif step[0] == "max_t":
                    n = step[1]
                    if n >= 2:
                        act.wait_ge(max_in[n - 2], 16 * SHIFT_ROWS)
                    rows = bank.bitcast(BF16)[0:SHIFT_ROWS * HALF, 0:GROUP]
                    drained(act.copy(max_row[:, n % 2, :], rows))
                    g, first = n // 2, HALF * (n % 2)
                    act.wait_ge(act_drained, act_slot[step] + 1)
                    for a in range(SHIFT_ROWS):
                        act.dma_start(q_stack[ROWS + a:ROWS + a + 1, first:first + HALF, g * GROUP:(g + 1) * GROUP],
                                      max_row[HALF * a:HALF * (a + 1), n % 2, :]).then_inc(max_in[n], 16)
                elif step[0] == "context":
                    n = step[1]
                    act.wait_ge(pv_done, last_batch[n] + 1)
                    if n >= 2:
                        act.wait_ge(vec_filled, vec_slot[("context_t", n - 2)] + 1)
                    act.copy(ctx_t[:, n % 2, :], ctx_ps[:, :]).then_inc(ctx_copied, 1)
                elif step[0] == "norm2_t":
                    g = step[1]
                    if g:
                        act.wait_ge(vec_filled, vec_slot[("ffn", g - 1)] + 1)
                    drained(act.activation(h2_t[:, :], bank, ACT.Identity,
                                           scale=mod_col[:, 3:4], bias=mod_col[:, 1:2]))
                elif step[0] == "logits":
                    g = step[1]
                    if g:
                        act.wait_ge(shift_ready, g)
                    drained(act.copy(logits[:, :, :], bank[:, 0:TG * NE].rearrange("p (t e) -> p t e", t=TG)))
                elif step[0] == "gate_shift":
                    g = step[1]
                    act.wait_ge(shift_ready, g + 1)
                    act.activation(gate_e[:, :, :], shifted[:, :, :], ACT.Exp).then_inc(gate_exp, 1)

        @block.vector
        def _(dve):
            chain = [0]

            def link(instruction):
                chain[0] += 1
                instruction.then_inc(vec_order, 1)
                dve.wait_ge(vec_order, chain[0])

            dve.memset(zeros[:, :], 0.0).then_inc(zeros_ready, 1)
            for step in steps:
                if step in vec_slot:
                    k = vec_slot[step]
                    banks = vec_ps[:, k % VEC_RING]
                    dve.wait_ge(vec_filled, k + 1)
                if step[0] == "maxima":
                    _, n, i, e, c = step
                    width = min(BANK, (TG * (n // 2) + i + 1) * P - c * BANK)
                    dve.tensor_reduce(part_max[:, n % 2, i, 2 * e:2 * e + 2, c], banks[:, :, 0:width], AX.X,
                                      ALU.max).then_inc(vec_drained, 1)
                elif step[0] in ("stats", "stats2"):
                    g, k = step[1], norm_no[step]
                    if step[0] == "stats":
                        dve.wait_ge(x_in_sem[g], 16)
                    for t in range(TG):
                        instruction = dve.bn_stats(bn[:, t, :], x_sb[:, TG * g + t, :])
                    link(instruction)
                    if k >= 2:
                        dve.wait_ge(rstd_ready, k - 1)
                    for t in range(TG):
                        instruction = dve.bn_aggr(mean_var[:, k % 2, t, :], bn[:, t, :])
                    link(instruction)
                    dve.tensor_scalar(var_eps[:, k % 2, :], mean_var[:, k % 2, :, 1], EPS, None,
                                      ALU.add).then_inc(var_ready, 1)
                elif step[0] == "silu":
                    dve.wait_ge(exp_c, 1)
                    link(dve.tensor_scalar(silu[:, 1:2], silu[:, 0:1], 1.0, None, ALU.add))
                    link(dve.reciprocal(silu[:, 2:3], silu[:, 1:2]))
                    link(dve.tensor_tensor(silu[:, 3:4], c_col[:, :], silu[:, 2:3], ALU.mult))
                    dve.wait_ge(const_ready, CONSTS["ones"])
                    dve.tensor_scalar(silu_wide[:, :], ones[:, :], silu[:, 3:4], None, ALU.mult).then_inc(silu_ready, 1)
                elif step[0] == "modulation":
                    dve.tensor_copy(gate_raw[:, :, :], banks[:, 1, 0:2 * D].rearrange("p (g d) -> p g d", g=2))
                    dve.tensor_copy(mod_col[:, 0:2], banks[:, 0, 0:2])
                    dve.tensor_scalar(mod_col[:, 2:4], banks[:, 0, 2:4], 1.0, None, ALU.add).then_inc(vec_drained, 1)
                elif step[0] == "gates":
                    dve.wait_ge(vec_drained, vec_slot[("modulation",)] + 1)
                    link(dve.tensor_scalar(gate_sign[:, :, :], gate_raw[:, :, :], 0.0, 2.0, ALU.is_ge, ALU.mult))
                    link(dve.tensor_scalar(gate_sign[:, :, :], gate_sign[:, :, :], -1.0, None, ALU.add))
                    link(dve.scalar_tensor_tensor(gate_size[:, :, :], gate_raw[:, :, :], -1.0, gate_raw[:, :, :],
                                                  ALU.mult, ALU.max))
                    link(dve.scalar_tensor_tensor(gates[:, :, :], gate_size[:, :, :], GATE_FLOOR, gate_sign[:, :, :],
                                                  ALU.max, ALU.mult))
                    dve.wait_ge(act_drained, act_slot[("weights",)] + 1)
                    dve.tensor_tensor(wv_gated[:, :], w_t[:, 2, :], gates[:, 0, :],
                                      ALU.mult).then_inc(gates_ready, 1)
                elif step[0] == "expert_out":
                    dve.tensor_tensor(ffn_w[:, :, :], banks[:, 0, 0:2 * D].rearrange("p (e d) -> p e d", e=2),
                                      gates[:, 1:2, :].broadcast_to([P, 2, D]), ALU.mult).then_inc(vec_drained, 1)
                elif step[0] == "project":
                    g = step[1]
                    cols = slice(g * GROUP, (g + 1) * GROUP)
                    dve.wait_ge(piece_ready[0], g + 1)
                    if g:
                        dve.wait_ge(piece_ready[2], g)
                    dve.tensor_tensor(left[:, :, :], banks, piece[0][:, :, cols],
                                      ALU.subtract).then_inc(vec_drained, 1)
                elif step[0] == "middle" and step[1] == 0:
                    dve.wait_ge(vec_drained, vec_slot[("project", 0)] + 1)
                    dve.tensor_copy(piece[1][:, :, 0:GROUP], left[:, :, :]).then_inc(piece_ready[1], 1)
                    dve.wait_ge(piece_ready[1], 1)
                    dve.tensor_tensor(piece[2][:, :, 0:GROUP], left[:, :, :], piece[1][:, :, 0:GROUP],
                                      ALU.subtract).then_inc(piece_ready[2], 1)
                elif step[0] == "max_sum":
                    n = step[1]
                    g = n // 2
                    dve.wait_ge(vec_drained, vec_slot[("maxima", n, TG - 1, HALF // 2 - 1, g)] + 1)
                    link(dve.tensor_reduce(neg_max[:, :], part_max[:, n % 2, :, :, 0:g + 1].rearrange(
                        "p i e c -> p (i e) c"), AX.X, ALU.max, negate=True))
                    whole = neg_max[:, :].rearrange("p (i e) -> p i e", e=HALF)
                    pieces = max_piece[:, n % 2]
                    if n >= 2:
                        dve.wait_ge(act_filled, act_slot[("max_t", n - 2)] + 1)
                    link(dve.tensor_copy(pieces[:, :, 0, :], whole))
                    dve.tensor_tensor(pieces[:, :, 1, :], whole, pieces[:, :, 0, :],
                                      ALU.subtract).then_inc(max_ready, 1)
                    dve.wait_ge(max_ready, n + 1)
                elif step[0] == "context_t":
                    n = step[1]
                    g, first = n // 2, (n % 2) * HALF * HD
                    heads = banks[:, 0, :].rearrange("p (t h v) -> p t h v", t=TG, h=HALF)
                    link(dve.reciprocal(sum_inv[:, :, :], heads[:, :, :, HD]))
                    dve.tensor_tensor(ctx_norm[:, :, :].rearrange("p t (h d) -> p t h d", h=HALF),
                                      heads[:, :, :, 0:HD],
                                      sum_inv[:, :, :].unsqueeze(3).broadcast_to([P, TG, HALF, HD]),
                                      ALU.mult).then_inc(vec_drained, 1)
                    dve.wait_ge(vec_drained, k + 1)
                    part = x_sb[:, TG * g:TG * g + TG, first:first + HALF * HD]
                    link(dve.tensor_tensor(part, part, ctx_norm[:, :, :], ALU.add))
                elif step[0] == "gate_shift":
                    g = step[1]
                    dve.wait_ge(act_drained, act_slot[("logits", g)] + 1)
                    link(dve.tensor_reduce(top[:, :], logits[:, :, :], AX.X, ALU.max))
                    dve.tensor_tensor(shifted[:, :, :], logits[:, :, :],
                                      top[:, :].unsqueeze(2).broadcast_to([P, TG, NE]),
                                      ALU.subtract).then_inc(shift_ready, 1)
                elif step[0] == "gate":
                    g = step[1]
                    dve.wait_ge(gate_exp, g + 1)
                    link(dve.tensor_reduce(gate_sum[:, :], gate_e[:, :, :], AX.X, ALU.add))
                    link(dve.reciprocal(gate_inv[:, :], gate_sum[:, :]))
                    link(dve.tensor_tensor(gate_p[:, :, :], gate_e[:, :, :],
                                           gate_inv[:, :].unsqueeze(2).broadcast_to([P, TG, NE]), ALU.mult))
                    link(dve.tensor_scalar(flags[:, :, :], gate_p[:, :, :], TOP_P, None, ALU.is_gt))
                    link(dve.tensor_reduce(count[:, :, 1], flags[:, :, :], AX.X, ALU.add))
                    link(dve.tensor_scalar(count[:, :, 0], count[:, :, 1], -1.0, float(NE), ALU.mult, ALU.add))
                    link(dve.tensor_tensor(expert_scale[:, :, :], count[:, :, :], gate_p[:, :, 0:2], ALU.mult))
                elif step[0] == "ffn":
                    g = step[1]
                    if g >= 2:
                        dve.wait_ge(out_stored[g - 2], 16)
                    flat = banks.rearrange("p b (t e d) -> p (b t) e d", t=TG // 2, e=2)
                    for t in range(TG):
                        instruction = dve.scalar_tensor_tensor(
                            result[:, g % 2, t, :], flat[:, t, 0, :], expert_scale[:, t, 0:1], x_sb[:, TG * g + t, :],
                            ALU.mult, ALU.add)
                    link(instruction)
                    for t in range(TG):
                        instruction = dve.scalar_tensor_tensor(
                            result[:, g % 2, t, :], flat[:, t, 1, :], expert_scale[:, t, 1:2], result[:, g % 2, t, :],
                            ALU.mult, ALU.add)
                        if t == TG - 2:
                            instruction.then_inc(vec_order, 1)
                            chain[0] += 1
                            dve.wait_ge(vec_order, chain[0])
                    instruction.then_inc(vec_drained, 1)

        @block.tensor
        def _(pe):
            def wait_spread(h):
                pe.wait_ge(act_drained, act_slot[("spread", h, 0)] + 1)

            for step in steps:
                if step in act_slot:
                    k = act_slot[step]
                    bank = act_ps[:, k % ACT_RING, :]
                    filled = act_filled
                    if k >= ACT_RING:
                        pe.wait_ge(act_drained, k - ACT_RING + 1)
                if step in vec_slot:
                    k = vec_slot[step]
                    banks = vec_ps[:, k % VEC_RING]
                    filled = vec_filled
                    if k >= VEC_RING:
                        pe.wait_ge(vec_drained, k - VEC_RING + 1)
                last = None
                if step[0] == "scores":
                    _, b, e = step
                    n, j = batches[b]
                    g, h, q0 = n // 2, HALF * (n % 2) + e, first_query(b)
                    if j == 0 and e == 0:
                        pe.wait_ge(max_in[n], 16 * SHIFT_ROWS)
                        if n == 0:
                            pe.wait_ge(ones_in, 16)
                    rows = ROWS + SHIFT_ROWS
                    if g == 0 and j == 0:
                        wait_spread(h)
                    last = pe.matmul(bank[:, q0:], k_stack[0:rows, h, j * P:(j + 1) * P],
                                     q_stack[0:rows, h, g * GROUP + q0:(g + 1) * GROUP], start=True, stop=True)
                elif step[0] == "maxima":
                    _, n, i, e, c = step
                    g = n // 2
                    tile = TG * g + i
                    if g and i == 0:
                        pe.wait_ge(stack_in[g], 16 * 2 * NPR)
                    width = min(BANK, (tile + 1) * P - c * BANK)
                    for m in range(2):
                        h = HALF * (n % 2) + 2 * e + m
                        if g == 0 and i == 0:
                            wait_spread(h)
                        last = pe.matmul(banks[:, m, 0:width], q_stack[0:ROWS, h, tile * P:(tile + 1) * P],
                                         k_stack[0:ROWS, h, c * BANK:c * BANK + width],
                                         start=True, stop=c < g)
                    if c == g:
                        pe.wait_ge(const_ready, CONSTS["mask"])
                        for m in range(2):
                            last = pe.matmul(banks[:, m, width - P:width], ident_bf[:, :], mask[:, :],
                                             start=False, stop=True)
                elif step[0] == "probs_v":
                    b = step[1]
                    n, j = batches[b]
                    g, q0 = n // 2, first_query(b)
                    pe.wait_ge(act_drained, act_slot[("scores", b, HALF - 1)] + 1)
                    if b in diagonal:
                        pe.wait_ge(masked, masks_until(b))
                    if j % TG == 0 and n % 2 == 0 and j // TG == g:
                        pe.wait_ge(act_drained, act_slot[("values", g)] + 1)
                    if j == 0 and n:
                        pe.wait_ge(ctx_copied, n)
                    for e in range(HALF):
                        last = pe.matmul(ctx_ps[VW * e:VW * e + VW, q0:], v_aug[:, j, HALF * (n % 2) + e, :],
                                         probs[:, b % PROB_BUFS, e, q0:], start=(j == 0),
                                         stop=(j == TG * g + TG - 1))
                    filled = pv_done
                elif step[0] == "warm":
                    pe.wait_ge(zeros_ready, 1)
                    for m in range(step[1]):
                        pe.matmul(ctx_ps[:, :], zeros[:, 0:P], zeros[:, :], start=True, stop=True)
                elif step[0] == "spread":
                    _, h, qk = step
                    pe.wait_ge(const_ready, CONSTS["spread"])
                    for m in range(3):
                        pe.wait_ge(piece_ready[m], 1)
                        last = pe.matmul(bank[0:ROWS, :], spread[:, qk, m, h].rearrange("p r d -> p (r d)"),
                                         piece[m][:, qk, 0:GROUP], start=m == 0, stop=m == 2)
                elif step[0] == "weights":
                    pe.wait_ge(const_ready, CONSTS["ident"])
                    pe.wait_ge(w_in, 16 * 5)
                    for w in range(3):
                        last = pe.transpose(bank[:, w * D:(w + 1) * D], w_sb[:, w, :], ident[:, :])
                elif step[0] == "ffn_weights":
                    pe.transpose(bank[:, 0:D], w_sb[:, 3, :], ident[:, :])
                    last = pe.transpose(bank[:, D:D + NE], gate_w[:, :], ident[0:NE, 0:NE])
                elif step[0] == "modulation":
                    pe.wait_ge(silu_ready, 1)
                    pe.wait_ge(mod_in, 16)
                    for m, s in enumerate((0, 3, 1, 4)):
                        pe.matmul(banks[:, 0, m:m + 1], wmod[:, s, :], silu[:, 3:4], start=True, stop=True)
                    for m, s in enumerate((2, 5)):
                        last = pe.matmul(banks[:, 1, m * D:(m + 1) * D], silu_wide[:, :], wmod[:, s, :],
                                         start=True, stop=True)
                elif step[0] == "expert_out":
                    pe.wait_ge(expert_in, 16)
                    pe.wait_ge(act_drained, act_slot[("ffn_weights",)] + 1)
                    for m in range(2):
                        last = pe.matmul(banks[:, 0, m * D:(m + 1) * D], expert_w[:, m, :], out_w_t[:, :],
                                         start=True, stop=True)
                elif step[0] in ("norm_t", "norm2_t"):
                    m = norm_no[("stats" + step[0][4:-2], step[1])]
                    for t in range(TG):
                        pe.wait_ge(norm_ready, TG * m + t + 1)
                        last = pe.transpose(bank[:, t * P:(t + 1) * P], normed[:, m % 2, t, :], ident[:, :])
                elif step[0] == "project":
                    g = step[1]
                    pe.wait_ge(act_drained, act_slot[("norm_t", g)] + 1)
                    for qk in range(2):
                        last = pe.matmul(banks[:, qk, :], w_t[:, qk, :], h_t[:, g * GROUP:(g + 1) * GROUP],
                                         start=True, stop=True)
                elif step[0] == "values":
                    g = step[1]
                    pe.wait_ge(gates_ready, 1)
                    for t in range(TG):
                        last = pe.matmul(bank[:, t * D:(t + 1) * D], h_t[:, (TG * g + t) * P:(TG * g + t + 1) * P],
                                         wv_gated[:, :], start=True, stop=True)
                elif step[0] == "max_t":
                    n = step[1]
                    pe.wait_ge(max_ready, n + 1)
                    rows = bank.bitcast(BF16)
                    for i in range(TG):
                        last = pe.transpose(rows[0:SHIFT_ROWS * HALF, i * P:(i + 1) * P],
                                            max_piece[:, n % 2, i].rearrange("p a e -> p (a e)"), ident_bf[:, :])
                elif step[0] == "context_t":
                    n = step[1]
                    pe.wait_ge(ctx_copied, n + 1)
                    for t in range(TG):
                        last = pe.transpose(banks[:, 0, t * P:(t + 1) * P], ctx_t[:, n % 2, t * P:(t + 1) * P],
                                            ident[:, :])
                elif step[0] == "logits":
                    g = step[1]
                    pe.wait_ge(act_drained, act_slot[("norm2_t", g)] + 1)
                    for t in range(TG):
                        last = pe.matmul(bank[:, t * NE:(t + 1) * NE], h2_t[:, t * P:(t + 1) * P], gate_w_t[:, :],
                                         start=True, stop=True)
                elif step[0] == "ffn":
                    g = step[1]
                    for t in range(TG):
                        last = pe.matmul(banks[:, t // 2, (t % 2) * 2 * D:(t % 2 + 1) * 2 * D],
                                         h2_t[:, t * P:(t + 1) * P], ffn_w[:, :, :].rearrange("p e d -> p (e d)"),
                                         start=True, stop=True)
                if last is not None:
                    last.then_inc(filled, 1)


_INS = ["L0_attn_hidden_states", "L0_attn_Wq", "L0_attn_Wk", "L0_attn_Wv", "L0_ffn_gate_W", "L0_ffn_expert_W",
        "L0_ffn_out_W", "L0_c", "L0_wmod"]


def kernel(**inputs):
    import numpy as np
    import concourse.bacc as bacc
    from concourse.bass_utils import run_bass_kernel_spmd

    nc = bacc.Bacc("TRN2", target_bir_lowering=False, num_devices=1)
    arrays, args = {}, []
    for name in _INS:
        a = np.ascontiguousarray(inputs[name])
        arrays[f"in_{name}"] = a
        args.append(nc.dram_tensor(f"in_{name}", a.shape, mybir.dt.from_np(a.dtype), kind="ExternalInput").ap())
    out = nc.dram_tensor("out_x", (1, S, D), F32, kind="ExternalOutput").ap()
    block_kernel(nc, *args, out)
    r = run_bass_kernel_spmd(nc, [arrays], core_ids=[0])
    return r.results[0]["out_x"]
```

```python
from contextlib import ExitStack

import concourse.bass as bass
from concourse import mybir

F32 = mybir.dt.float32
BF16 = mybir.dt.bfloat16
ALU = mybir.AluOpType
ACT = mybir.ActivationFunctionType
AX = mybir.AxisListType

P = 128
S, D = 2048, 128
NH = 8
HD = D // NH
NE = 8
TOP_P = 0.3
EPS = 1e-5
GATE_FLOOR = 0.25
NT = S // P
TG = 4
GROUP = TG * P
NG = S // GROUP
HALF = 4
BLOCKS = [(0, 4), (4, 4), (8, 4), (12, 2), (14, 2)]
NB = len(BLOCKS)
GATE_STEPS = 6
NI = 2 * NB
VW = 32
PRODUCTS = [(0, 0), (0, 1), (0, 2), (1, 0), (1, 1), (1, 2), (2, 0)]
NPR = len(PRODUCTS)
ROWS = NPR * HD
SHIFT_ROWS = 2
SCORE_SCALE = HD ** -0.5
MASKED = -(2.0 ** 100)
BANKS = 7
PROB_BUFS = 4
PREPARED_AFTER = {2: 1, 3: 2}
WARM = (11, 1, 2, 8)

FILL_TO_TAKE = 250
TAKE_TO_FILL = 360
ROWS_TO_SCORES = 1500
STACKS_TO_MAXIMA = 1800
PROBS_V_PASSES = 500
KEEP_PAIR = 50
FIRST_ROWS_EARLY = 300
BIAS = (0, 0, 0, 0, 400, 0)
BACKLOG = {"act": 0.45, "vec": 0.15, "pool": 0, "sp": 0}
BANK = 512

ACT_STAGES = {"spread", "weights", "ffn_weights", "norm_t", "values", "max_t", "scores", "norm2_t"}
VEC_STAGES = {"modulation", "expert_out", "project", "maxima", "context_t", "logits", "ffn"}
PAIR_STAGES = {"modulation", "maxima", "ffn"}


def item_batches():
    return [(n, j) for n in range(NI) for j in range(sum(BLOCKS[n // 2]))]


def score_width(n, j):
    first, tiles = BLOCKS[n // 2]
    return (tiles - max(0, j - first)) * P


def maxima_width(n, i, c):
    return min(BANK, (BLOCKS[n // 2][0] + i + 1) * P - c * BANK)


def score_slots(n):
    return BLOCKS[n // 2][1]


def key_chunks(n):
    return BLOCKS[n // 2][0] // TG + 1


def maxima_units(n):
    return [("maxima", n, i, e, c) for i in range(BLOCKS[n // 2][1]) for e in range(HALF // 2)
            for c in range(key_chunks(n))]


def token_stats(name, k):
    return [("tile_stats", name, k), ("mean_var", name, k), (name, k)]


def stack_loads(g):
    return [("store", g)] + [("stack", g, r) for r in sorted(range(NPR), key=lambda r: 2 in PRODUCTS[r])]


def prepare(g):
    return (token_stats("stats", g) + [("normalize", g), ("norm_t", g), ("project", g, 1), ("project", g, 0),
                                       ("middle", g, 1), ("middle", g, 0)] + stack_loads(g) + [("values", g)])


def finish(k):
    return (token_stats("stats2", k) + [("normalize2", k), ("norm2_t", k), ("logits", k), ("gate_shift", k)]
            + [("gate", k, m) for m in range(GATE_STEPS)] + [("ffn", k)])


def estimate(s, batches):
    kind = s[0]
    if kind == "scores":
        n, j = batches[s[1]]
        w = score_width(n, j) * HALF // score_slots(n)
        mask = [("pool", 600)] if j >= BLOCKS[n // 2][0] and s[2] == score_slots(n) - 1 else []
        return w / 2.4 + 3, [("act", w / 1.2 + 51)] + mask, 200
    if kind == "maxima":
        w = maxima_width(s[1], s[2], s[4])
        return w / 1.2 + 6 + (110 if s[4] == key_chunks(s[1]) - 1 else 0), [("vec", 2 * w * 1.042 + 65)], 200
    if kind == "probs_v":
        return score_width(*batches[s[1]]) * 4 / 2.4 + 80, [], PROBS_V_PASSES
    if kind == "middle":
        return 0, [("act", 520), ("pool", 1113) if s[1] else ("vec", 600)], 200
    if kind == "warm":
        return 213 * s[1], [], 0
    pe, takers, passes = {
        "silu": (0, [("vec", 1100)], 200), "spread_zeros": (0, [("pool", 2300)], 0),
        "spread_rows": (0, [("pool", 4400)], 0),
        "constants": (0, [("pool", 6800)], 0),
        "weights": (330, [("act", 370)], 200), "ffn_weights": (110, [("act", 220)], 200),
        "modulation": (440, [("vec", 470)], 200), "expert_out": (430, [("vec", 340)], 200),
        "gates": (0, [("vec", 1300)], 200), "spread": (640, [("act", 480)], 200),
        "tile_stats": (0, [("vec", 800)], 100), "mean_var": (0, [("vec", 300)], 100),
        "stats": (0, [("vec", 150), ("pool", 1000)], 200), "stats2": (0, [("vec", 150), ("pool", 1000)], 200),
        "normalize": (0, [("act", 1600)], 200), "normalize2": (0, [("act", 1600)], 200),
        "norm_t": (430, [("act", 620)], 200), "norm2_t": (430, [("act", 620)], 200),
        "project": (855, [("act", 480), ("vec", 600)], 200), 
        "values": (860, [("act", 480)], 200),
        "max_reduce": (0, [("vec", 100)], 100), "max_high": (0, [("vec", 80)], 100),
        "max_sum": (0, [("vec", 90)], 100), "context_add": (0, [("vec", 350)], 100),
        "max_t": (220, [("act", 480), ("sp", 1200)], ROWS_TO_SCORES),
        "store": (0, [("sp", 1700)], 2400), "stack": (0, [("sp", 950)], 0), "context": (0, [("act", 480)], 200),
        "context_t": (430, [("vec", 650)], 200), "logits": (30, [("vec", 450)], 300),
        "gate_shift": (0, [("act", 200)], 200), "gate": (0, [("vec", 95)], 100),
        "ffn": (1720, [("vec", 2100)], 200)}[kind]
    if kind in ("context", "context_t", "context_add"):
        share = BLOCKS[s[1] // 2][1] / TG
    elif kind in ("tile_stats", "mean_var") and s[1] == "stats2":
        share = BLOCKS[s[2]][1] / TG
    elif kind in ("normalize2", "norm2_t", "ffn"):
        share = BLOCKS[s[1]][1] / TG
    else:
        share = 1
    return pe * share, [(engine, ns * share) for engine, ns in takers], passes


def plan():
    batches = item_batches()
    maxima = [maxima_units(n) for n in range(NI)]
    last_batch = {n: b for b, (n, _) in enumerate(batches)}
    fixed = [("warm", WARM[0]), ("spread_zeros",)] + token_stats("stats", 0)
    fixed += [("silu",), ("normalize", 0), ("weights",), ("modulation",), ("ffn_weights",), ("spread_rows",)]
    fixed += token_stats("stats", 1)
    fixed += [("gates",), ("warm", WARM[1]),
             ("norm_t", 0), ("warm", WARM[2]), ("project", 0, 1), ("project", 0, 0), ("constants",),
             ("middle", 0, 1), ("middle", 0, 0), ("normalize", 1), ("expert_out",), ("warm", WARM[3])]
    spreads = [("spread", h, qk) for h in range(NH) for qk in (1, 0)]
    by_pair = [[m for m in maxima[n] if m[3] == e] for n in range(2) for e in range(2)]
    fixed += spreads[0:4] + [("norm_t", 1)] + spreads[4:6]
    fixed += [("project", 1, 1), ("project", 1, 0), ("middle", 1, 1), ("middle", 1, 0)]
    for m, spread in zip(by_pair[0], spreads[6:8] + spreads[8:10]):
        fixed += [m, spread]
    fixed += stack_loads(1)[:1]
    for m, spread in zip(by_pair[1], spreads[10:12] + [("values", 0), ("values", 1)]):
        fixed += [m, spread]
    maxima_stream = by_pair[2] + spreads[12:16] + by_pair[3] + [m for n in range(2, NI) for m in maxima[n]]
    streams = [[], [(name, n) for n in range(NI) for name in ("max_reduce", "max_high", "max_sum", "max_t")],
               stack_loads(1)[1:] + prepare(2) + prepare(3), maxima_stream,
               [("probs_v", b) for b in range(len(batches))],
               [("scores", b, e) for b, (n, _) in enumerate(batches) for e in range(score_slots(n))]]

    before = {("tile_stats", "stats", g): ("max_sum", n) for g, n in PREPARED_AFTER.items()}
    for n in range(NI):
        before[("max_reduce", n)] = maxima[n][-1]
        before[("max_high", n)] = ("max_reduce", n)
        before[("max_sum", n)] = ("max_high", n)
        before[("max_t", n)] = ("max_sum", n)
        before[("context", n)] = ("probs_v", last_batch[n])
        before[("context_t", n)] = ("context", n)
    for n in range(NI):
        before[("context_add", n)] = ("context_t", n)
    for chain in [[("context_add", 2 * k + 1)] + finish(k) for k in range(NB)] + [prepare(g) for g in range(NG)]:
        before |= dict(zip(chain[1:], chain[:-1]))
    for g in range(NG):
        before[("values", g)] = ("norm_t", g)

    order, banks, last_users = [], {}, {}
    done, now = {}, {"pe": 0.0, "act": 0.0, "vec": 0.0, "pool": 0.0, "sp": 0.0}
    empty = [0.0] * BANKS
    user = [None] * BANKS

    def ready(s):
        if s[0] == "scores":
            needs = [("max_t", batches[s[1]][0])] + ([("probs_v", s[1] - PROB_BUFS)] if s[1] >= PROB_BUFS else [])
        elif s[0] == "probs_v":
            n, j = batches[s[1]]
            needs = [("scores", s[1], score_slots(n) - 1)] + ([("context", n - 1)] if n and j == 0 else [])
        elif s[0] == "maxima":
            chunk = key_chunks(s[1]) - 1
            needs = [stack_loads(chunk)[-1] if chunk else ("middle", 0, 0)]
            needs += [("max_reduce", s[1] - 2)] if s[1] >= 2 else []
            needs += [("spread", NH - 1, 0)] if s[1] == 1 and s[3] == 1 else []
        else:
            needs = [before[s]] if s in before else []
        if any(m not in done for m in needs):
            return None
        if s[0] == "stack":
            return max(done[needs[0]], now["sp"] - 500)
        late = STACKS_TO_MAXIMA if s[0] == "maxima" and chunk else 0
        return max([done[m] for m in needs] + [0.0]) + late

    def choose_banks(s):
        if s[0] in PAIR_STAGES:
            first = min(range(0, BANKS - 1, 2), key=lambda b: max(empty[b:b + 2]))
            return [first, first + 1]
        if s[0] in ACT_STAGES or s[0] in VEC_STAGES:
            def cost_of(b):
                at = max(empty[b], now["pe"])
                return at + (KEEP_PAIR if b < BANKS - 1 and empty[b ^ 1] <= now["pe"] else 0), empty[b]
            return [min(range(BANKS), key=cost_of)]
        return []

    def place(s, start, used):
        on_pe, takers, passes = estimate(s, batches)
        end = taken_out = start + on_pe
        if on_pe:
            now["pe"] = end
        for engine, ns in takers:
            hears = FILL_TO_TAKE if on_pe or engine in ("pool", "sp") else 0
            now[engine] = end = max(now[engine], end + hears) + ns
            if engine not in ("pool", "sp"):
                taken_out = end
        banks[s] = used
        last_users[s] = [user[b] for b in used if user[b] is not None]
        for b in used:
            empty[b], user[b] = taken_out + TAKE_TO_FILL, s
        done[s] = end + passes
        order.append(s)

    for s in fixed:
        used = choose_banks(s)
        on_pe = estimate(s, batches)[0] > 0
        place(s, max([ready(s) or 0.0, now["pe"] if on_pe else 0.0] + [empty[b] for b in used]), used)
    while any(streams):
        options = []
        for rank, stream in enumerate(streams):
            if stream and (at := ready(stream[0])) is not None:
                s = stream[0]
                used = choose_banks(s)
                start = max([at, now["pe"]] + [empty[b] for b in used])
                takers = estimate(s, batches)[1]
                backlog = max(0.0, now[takers[0][0]] - start) * BACKLOG[takers[0][0]] if takers else 0.0
                early = FIRST_ROWS_EARLY if s[1:] == (0,) and s[0] in ("max_reduce", "max_high", "max_sum") else 0
                options.append((start + BIAS[rank] + backlog - early, rank, start, used))
        _, rank, start, used = min(options)
        s = streams[rank].pop(0)
        place(s, start, used)
        if s[0] == "probs_v" and last_batch[batches[s[1]][0]] == s[1]:
            n = batches[s[1]][0]
            streams[0] += [("context", n), ("context_t", n), ("context_add", n)] + (finish(n // 2) if n % 2 else [])
    return order, banks, last_users


def block_kernel(nc, x_in, wq_in, wk_in, wv_in, gate_w_in, expert_w_in, out_w_in, c_in, wmod_in, out):
    steps, banks_of, last_users = plan()
    batches = item_batches()
    last_batch = {n: b for b, (n, _) in enumerate(batches)}
    act_slot = {s: k for k, s in enumerate([s for s in steps if s[0] in ACT_STAGES])}
    vec_slot = {s: k for k, s in enumerate([s for s in steps if s[0] in VEC_STAGES])}
    diagonal = [b for b, (n, j) in enumerate(batches) if j >= BLOCKS[n // 2][0]]

    def first_query(b):
        n, j = batches[b]
        return max(0, j - BLOCKS[n // 2][0]) * P

    def masks_until(b):
        return sum(1 for d in diagonal if d <= b)

    with ExitStack() as ctx:
        def sb(name, shape, dt):
            return ctx.enter_context(nc.sbuf_tensor(name, shape, dt))

        def sem(name):
            return ctx.enter_context(nc.semaphore(name))

        ps = ctx.enter_context(nc.psum_tensor("ps", [P, BANKS, BANK], F32))
        ctx_ps = ctx.enter_context(nc.psum_tensor("ctx_ps", [P, BANK], F32))

        x_sb = sb("x_sb", [P, NT, D], F32)
        w_sb = sb("w_sb", [P, 4, D], F32)
        w_t = sb("w_t", [P, 3, D], F32)
        wv_gated = sb("wv_gated", [P, D], F32)
        out_w_t = sb("out_w_t", [P, D], F32)
        gate_w = sb("gate_w", [NE, D], F32)
        gate_w_t = sb("gate_w_t", [P, NE], F32)
        expert_w = sb("expert_w", [P, 2, D], F32)
        ffn_w = sb("ffn_w", [P, 2, D], F32)
        c_col = sb("c_col", [P, 1], F32)
        silu = sb("silu", [P, 4], F32)
        silu_wide = sb("silu_wide", [P, P], F32)
        wmod = sb("wmod", [P, 6, D], F32)
        mod_col = sb("mod_col", [P, 4], F32)
        gates = sb("gates", [P, 2, D], F32)
        gate_raw = sb("gate_raw", [P, 2, D], F32)
        gate_sign = sb("gate_sign", [P, 2, D], F32)
        gate_size = sb("gate_size", [P, 2, D], F32)
        ident = sb("ident", [P, P], F32)
        ident_bf = sb("ident_bf", [P, P], BF16)
        mask = sb("mask", [P, P], BF16)
        ones = sb("ones", [P, P], F32)
        ones_row = sb("ones_row", [2, S], BF16)
        zeros = sb("zeros", [P, BANK], BF16)
        half_neg = sb("half_neg", [P, TG], F32)
        bn = sb("bn", [P, 2, TG, 6], F32)
        mean_var = sb("mean_var", [P, 2, TG, 2], F32)
        var_eps = sb("var_eps", [P, 2, TG], F32)
        neg_mean = sb("neg_mean", [P, 2, TG], F32)
        rstd = sb("rstd", [P, 2, TG], F32)
        norm_shift = sb("norm_shift", [P, 2, TG], F32)
        normed = sb("normed", [P, 2, TG, D], F32)
        h_t = sb("h_t", [P, S], F32)
        piece = [sb(f"piece{k}", [P, 2, S], BF16) for k in range(3)]
        left = sb("left", [P, 2, GROUP], F32)
        q_stack = sb("q_stack", [P, NH, S], BF16)
        k_stack = sb("k_stack", [P, NH, S], BF16)
        v_aug = sb("v_aug", [P, NT, NH, VW], F32)
        part_max = sb("part_max", [P, 2, TG, HALF, NG], F32)
        neg_max = sb("neg_max", [P, TG * HALF], F32)
        max_piece = sb("max_piece", [P, 2, TG, SHIFT_ROWS, HALF], BF16)
        max_row = sb("max_row", [SHIFT_ROWS * HALF, 2, GROUP], BF16)
        spread = sb("spread", [P, 2, 3, NH, NPR, HD], BF16)
        probs = sb("probs", [P, PROB_BUFS, HALF, GROUP], F32)
        ctx_t = sb("ctx_t", [P, 2, GROUP], F32)
        ctx_norm = sb("ctx_norm", [P, TG, HALF * HD], F32)
        sum_inv = sb("sum_inv", [P, TG, HALF], F32)
        h2_t = sb("h2_t", [P, GROUP], F32)
        top = sb("top", [P, TG], F32)
        shifted = sb("shifted", [P, TG, NE], F32)
        gate_e = sb("gate_e", [P, TG, NE], F32)
        gate_sum = sb("gate_sum", [P, TG], F32)
        gate_inv = sb("gate_inv", [P, TG], F32)
        gate_p = sb("gate_p", [P, TG, NE], F32)
        flags = sb("flags", [P, TG, 2, NE], F32)
        count = sb("count", [P, TG, 2], F32)
        expert_scale = sb("expert_scale", [P, TG, 2], F32)
        result = sb("result", [P, 2, TG, D], F32)

        scratch = nc.dram_tensor("piece_scratch", (3, 2, D, S), BF16, kind="Internal").ap()

        x_in_sem = [sem(f"x_in{g}") for g in range(NG)]
        w_in = sem("w_in")
        c_loaded = sem("c_loaded")
        mod_in = sem("mod_in")
        expert_in = sem("expert_in")
        const_ready = sem("const_ready")
        ones_in = sem("ones_in")
        act_filled = sem("act_filled")
        act_drained = sem("act_drained")
        vec_filled = sem("vec_filled")
        vec_drained = sem("vec_drained")
        vec_order = sem("vec_order")
        zeros_ready = sem("zeros_ready")
        exp_c = sem("exp_c")
        silu_ready = sem("silu_ready")
        gates_ready = sem("gates_ready")
        var_ready = sem("var_ready")
        rstd_ready = sem("rstd_ready")
        pool_order = sem("pool_order")
        act_normed = sem("act_normed")
        vec_normed = sem("vec_normed")
        piece_ready = [sem(f"piece_ready{k}") for k in range(3)]
        stored = [sem(f"stored{g}") for g in range(NG)]
        stored_lo = [sem(f"stored_lo{g}") for g in range(NG)]
        stack_in = [sem(f"stack_in{g}") for g in range(NG)]
        max_ready = sem("max_ready")
        max_in = [sem(f"max_in{n}") for n in range(NI)]
        masked = sem("masked")
        pv_done = sem("pv_done")
        ctx_copied = sem("ctx_copied")
        gate_exp = sem("gate_exp")
        out_stored = [sem(f"out_stored{k}") for k in range(NB)]

        CONSTS = dict(ident=2, ones=3, half_neg=4, spread=5 + 2 * NPR, ident_bf=7 + 2 * NPR,
                      mask=9 + 2 * NPR, ones_row=10 + 2 * NPR, v_one=12 + 2 * NPR)
        norms = [s for s in steps if s[0] in ("stats", "stats2")]
        norm_no = {s: k for k, s in enumerate(norms)}
        norm_tiles = [(TG * m, TG) if name == "stats" else BLOCKS[m] for name, m in norms]
        by_vec_norm = [s in (("stats", 0), ("stats", 1), ("stats2", NB - 1)) for s in norms]

        def wait_normed(engine, k, tiles):
            before = sum(norm_tiles[m][1] for m in range(k) if by_vec_norm[m] == by_vec_norm[k])
            engine.wait_ge(vec_normed if by_vec_norm[k] else act_normed, before + tiles)

        x_tiles = x_in.rearrange("b (t p) d -> p (b t) d", p=P)
        out_tiles = out.rearrange("b (t p) d -> p (b t) d", p=P)

        block = ctx.enter_context(nc.Block())

        @block.sync
        def _(sp):
            for g in range(NG):
                sp.dma_start(x_sb[:, TG * g:TG * g + TG, :],
                             x_tiles[:, TG * g:TG * g + TG, :]).then_inc(x_in_sem[g], 16)
                if g == 0:
                    for k, w in ((2, wv_in), (3, out_w_in)):
                        sp.dma_start(w_sb[:, k, :], w).then_inc(w_in, 16)
                    sp.dma_start(gate_w[:, :], gate_w_in).then_inc(w_in, 16)
            sp.dma_start(expert_w[:, :, :], expert_w_in[0:2].rearrange("e h d -> h e d")).then_inc(expert_in, 16)
            sp.wait_ge(const_ready, CONSTS["ones_row"])
            sp.dma_start(k_stack[ROWS:ROWS + SHIFT_ROWS, :, :],
                         ones_row[:, :].unsqueeze(1).broadcast_to([SHIFT_ROWS, NH, S])).then_inc(ones_in, 16)

            for step in steps:
                if step[0] == "store":
                    g = step[1]
                    cols = slice(g * GROUP, (g + 1) * GROUP)
                    for k in range(3):
                        sp.wait_ge(piece_ready[k], 2 * g + 2)
                        sp.dma_start(scratch[k, :, :, cols].rearrange("a p c -> p a c"),
                                     piece[k][:, :, cols]).then_inc(stored[g] if k < 2 else stored_lo[g], 16)
                elif step[0] == "stack":
                    _, g, r = step
                    cols = slice(g * GROUP, (g + 1) * GROUP)
                    sp.wait_ge(stored[g], 32)
                    if 2 in PRODUCTS[r]:
                        sp.wait_ge(stored_lo[g], 16)
                    for qk, stack in enumerate((q_stack, k_stack)):
                        sp.dma_start(stack[r * HD:(r + 1) * HD, :, cols],
                                     scratch[PRODUCTS[r][qk], qk, :, cols].rearrange("(h p) c -> p h c", p=HD)
                                     ).then_inc(stack_in[g], 16)
                elif step[0] == "max_t":
                    n = step[1]
                    (tile, tiles), first = BLOCKS[n // 2], HALF * (n % 2)
                    sp.wait_ge(act_drained, act_slot[step] + 1)
                    for a in range(SHIFT_ROWS):
                        sp.dma_start(q_stack[ROWS + a:ROWS + a + 1, first:first + HALF, tile * P:(tile + tiles) * P],
                                     max_row[HALF * a:HALF * (a + 1), n % 2, 0:tiles * P]).then_inc(max_in[n], 16)
                elif step[0] == "ffn":
                    first, tiles = BLOCKS[step[1]]
                    sp.wait_ge(vec_drained, vec_slot[step] + 1)
                    sp.dma_start(out_tiles[:, first:first + tiles, :],
                                 result[:, step[1] % 2, 0:tiles]).then_inc(out_stored[step[1]], 16)
            for k in range(NB):
                sp.wait_ge(out_stored[k], 16)

        @block.gpsimd
        def _(pool):
            pool.memset(ident[:, :], 0.0).then_inc(const_ready, 1)
            pool.wait_ge(const_ready, 1)
            pool.affine_select(out=ident[:, :], in_=ident[:, :], compare_op=ALU.not_equal, fill=1.0, base=0,
                               pattern=[[-1, P]], channel_multiplier=1).then_inc(const_ready, 1)
            pool.memset(ones[:, :], 1.0).then_inc(const_ready, 1)
            pool.memset(half_neg[:, :], -0.5).then_inc(const_ready, 1)

            for step in steps:
                if step[0] in ("stats", "stats2"):
                    k = norm_no[step]
                    if k == 0:
                        pool.wait_ge(const_ready, CONSTS["half_neg"])
                    pool.wait_ge(var_ready, k + 1)
                    if k >= 2:
                        wait_normed(pool, k - 2, norm_tiles[k - 2][1])
                    tiles = norm_tiles[k][1]
                    pool.tensor_tensor(rstd[:, k % 2, 0:tiles], var_eps[:, k % 2, 0:tiles], half_neg[:, 0:tiles],
                                       ALU.pow).then_inc(rstd_ready if by_vec_norm[k] else pool_order, 1)
                    if by_vec_norm[k]:
                        continue
                    pool.wait_ge(pool_order, k + 1 - sum(by_vec_norm[:k]))
                    pool.tensor_tensor(norm_shift[:, k % 2, 0:tiles], neg_mean[:, k % 2, 0:tiles],
                                       rstd[:, k % 2, 0:tiles], ALU.mult).then_inc(rstd_ready, 1)
                elif step[0] == "spread_zeros":
                    pool.memset(spread[:, :, :, :, :, :].rearrange("p a k h r d -> p (a k h r d)").bitcast(F32),
                                0.0).then_inc(const_ready, 1)
                elif step[0] == "spread_rows":
                    pool.wait_ge(const_ready, CONSTS["half_neg"] + 1)
                    for r, pair in enumerate(PRODUCTS):
                        for qk, k in enumerate(pair):
                            part = spread[:, qk, k, :, r, :]
                            pool.affine_select(out=part, in_=part, compare_op=ALU.not_equal, fill=1.0, base=0,
                                               pattern=[[-HD, NH], [-1, HD]],
                                               channel_multiplier=1).then_inc(const_ready, 1)
                elif step[0] == "constants":
                    pool.memset(ident_bf[:, :], 0.0).then_inc(const_ready, 1)
                    pool.wait_ge(const_ready, CONSTS["ident_bf"] - 1)
                    pool.affine_select(out=ident_bf[:, :], in_=ident_bf[:, :], compare_op=ALU.not_equal, fill=1.0,
                                       base=0, pattern=[[-1, P]], channel_multiplier=1).then_inc(const_ready, 1)
                    pool.memset(mask[:, :], 0.0).then_inc(const_ready, 1)
                    pool.wait_ge(const_ready, CONSTS["mask"] - 1)
                    pool.affine_select(out=mask[:, :], in_=mask[:, :], compare_op=ALU.is_ge, fill=MASKED, base=0,
                                       pattern=[[-1, P]], channel_multiplier=1).then_inc(const_ready, 1)
                    pool.memset(ones_row[:, :], 1.0).then_inc(const_ready, 1)
                    pool.memset(v_aug[:, :, :, :], 0.0).then_inc(const_ready, 1)
                    pool.wait_ge(const_ready, CONSTS["v_one"] - 1)
                    pool.memset(v_aug[:, :, :, HD:HD + 1], 1.0).then_inc(const_ready, 1)
                elif step[0] == "middle" and step[1]:
                    _, g, qk = step
                    cols = slice(g * GROUP, (g + 1) * GROUP)
                    pool.wait_ge(piece_ready[1], 2 * g + 2 - qk)
                    pool.tensor_tensor(piece[2][:, qk, cols], left[:, qk, :], piece[1][:, qk, cols],
                                       ALU.subtract).then_inc(piece_ready[2], 1)
                elif step[0] == "scores" and step[1] in diagonal and step[2] == score_slots(batches[step[1]][0]) - 1:
                    b = step[1]
                    q0 = first_query(b)
                    part = probs[:, b % PROB_BUFS, :, q0:q0 + P]
                    pool.wait_ge(act_drained, act_slot[step] + 1)
                    pool.affine_select(out=part, in_=part, compare_op=ALU.is_ge, fill=0.0, base=0,
                                       pattern=[[0, HALF], [1, P]], channel_multiplier=-1).then_inc(masked, 1)

        @block.scalar
        def _(act):
            def drained(instruction):
                instruction.then_inc(act_drained, 1)

            act.dma_start(c_col[:, :], c_in.rearrange("a d -> d a")).then_inc(c_loaded, 16)
            act.dma_start(wmod[:, :, :], wmod_in.rearrange("d (s n) -> d s n", s=6)).then_inc(mod_in, 16)
            for k, w in enumerate((wq_in, wk_in)):
                act.dma_start(w_sb[:, k, :], w).then_inc(w_in, 16)
            act.wait_ge(c_loaded, 16)
            act.activation(silu[:, 0:1], c_col[:, :], ACT.Exp, scale=-1.0).then_inc(exp_c, 1)
            for step in steps:
                if step in act_slot:
                    k = act_slot[step]
                    bank = ps[:, banks_of[step][0], :]
                    act.wait_ge(act_filled, k + 1)
                if step[0] == "scores":
                    _, b, e = step
                    n = batches[b][0]
                    q0, tiles = first_query(b), BLOCKS[n // 2][1]
                    heads = HALF // score_slots(n)
                    if b >= PROB_BUFS:
                        act.wait_ge(pv_done, b - PROB_BUFS + 1)
                    drained(act.activation(probs[:, b % PROB_BUFS, heads * e:heads * e + heads, q0:tiles * P],
                                           bank.rearrange("p (h q) -> p h q", h=heads)[:, :, q0:],
                                           ACT.Exp, scale=SCORE_SCALE))
                elif step[0] == "spread":
                    _, h, qk = step
                    drained(act.copy((q_stack, k_stack)[qk][0:ROWS, h, 0:GROUP], bank[0:ROWS, :]))
                elif step[0] == "weights":
                    drained(act.copy(w_t[:, :, :], bank[:, 0:3 * D].rearrange("p (w n) -> p w n", w=3)))
                elif step[0] == "ffn_weights":
                    act.copy(out_w_t[:, :], bank[:, 0:D])
                    drained(act.copy(gate_w_t[:, :], bank[:, D:D + NE]))
                elif step[0] in ("normalize", "normalize2") and not by_vec_norm[norm_no[("stats" + step[0][9:], step[1])]]:
                    k = norm_no[("stats" + step[0][9:], step[1])]
                    if k >= 2:
                        name, h = norms[k - 2]
                        act.wait_ge(act_filled, act_slot[("norm" + name[5:] + "_t", h)] + 1)
                    act.wait_ge(rstd_ready, k + 1)
                    first, tiles = norm_tiles[k]
                    for t in range(tiles):
                        act.activation(normed[:, k % 2, t, :], x_sb[:, first + t, :], ACT.Identity,
                                       scale=rstd[:, k % 2, t:t + 1],
                                       bias=norm_shift[:, k % 2, t:t + 1]).then_inc(act_normed, 1)
                elif step[0] == "middle":
                    _, g, qk = step
                    act.wait_ge(vec_drained, vec_slot[("project", g, qk)] + 1)
                    act.copy(piece[1][:, qk, g * GROUP:(g + 1) * GROUP], left[:, qk, :]).then_inc(piece_ready[1], 1)
                elif step[0] == "norm_t":
                    g = step[1]
                    act.wait_ge(vec_drained, vec_slot[("modulation",)] + 1)
                    drained(act.activation(h_t[:, g * GROUP:(g + 1) * GROUP], bank, ACT.Identity,
                                           scale=mod_col[:, 2:3], bias=mod_col[:, 0:1]))
                elif step[0] == "project":
                    _, g, qk = step
                    act.wait_ge(vec_filled, vec_slot[step] + 1)
                    act.copy(piece[0][:, qk, g * GROUP:(g + 1) * GROUP],
                             ps[:, banks_of[step][0], :]).then_inc(piece_ready[0], 1)
                elif step[0] == "values":
                    g = step[1]
                    act.wait_ge(const_ready, CONSTS["v_one"])
                    drained(act.copy(v_aug[:, TG * g:TG * g + TG, :, 0:HD],
                                     bank.rearrange("p (t h d) -> p t h d", t=TG, h=NH)))
                elif step[0] == "max_t":
                    n = step[1]
                    if n >= 2:
                        act.wait_ge(max_in[n - 2], 16 * SHIFT_ROWS)
                    tiles = BLOCKS[n // 2][1]
                    rows = bank.bitcast(BF16)[0:SHIFT_ROWS * HALF, 0:tiles * P]
                    drained(act.copy(max_row[:, n % 2, 0:tiles * P], rows))
                elif step[0] == "context":
                    n = step[1]
                    act.wait_ge(pv_done, last_batch[n] + 1)
                    if n >= 2:
                        act.wait_ge(vec_filled, vec_slot[("context_t", n - 2)] + 1)
                    queries = BLOCKS[n // 2][1] * P
                    act.copy(ctx_t[:, n % 2, 0:queries], ctx_ps[:, 0:queries]).then_inc(ctx_copied, 1)
                elif step[0] == "norm2_t":
                    g = step[1]
                    if g:
                        act.wait_ge(vec_filled, vec_slot[("ffn", g - 1)] + 1)
                    queries = BLOCKS[g][1] * P
                    drained(act.activation(h2_t[:, 0:queries], bank[:, 0:queries], ACT.Identity,
                                           scale=mod_col[:, 3:4], bias=mod_col[:, 1:2]))
                elif step[0] == "gate_shift":
                    g = step[1]
                    act.wait_ge(vec_drained, vec_slot[("logits", g)] + 1)
                    tiles = BLOCKS[g][1]
                    act.activation(gate_e[:, 0:tiles, :], shifted[:, 0:tiles, :], ACT.Exp).then_inc(gate_exp, 1)

        @block.vector
        def _(dve):
            chain = [0]
            made = {}

            def make(step, instruction):
                chain[0] += 1
                instruction.then_inc(vec_order, 1)
                made[step] = chain[0]

            def link(instruction):
                chain[0] += 1
                instruction.then_inc(vec_order, 1)
                dve.wait_ge(vec_order, chain[0])

            dve.memset(zeros[:, :], 0.0).then_inc(zeros_ready, 1)
            for step in steps:
                if step in vec_slot:
                    k = vec_slot[step]
                    banks = ps[:, banks_of[step][0]:banks_of[step][-1] + 1, :]
                    dve.wait_ge(vec_filled, k + 1)
                if step[0] == "maxima":
                    _, n, i, e, c = step
                    width = maxima_width(n, i, c)
                    dve.tensor_reduce(part_max[:, n % 2, i, 2 * e:2 * e + 2, c], banks[:, :, 0:width], AX.X,
                                      ALU.max).then_inc(vec_drained, 1)
                elif step[0] == "tile_stats":
                    k = norm_no[step[1:]]
                    first, tiles = norm_tiles[k]
                    if step[1] == "stats":
                        dve.wait_ge(x_in_sem[step[2]], 16)
                    else:
                        dve.wait_ge(vec_order, made[("context_add", 2 * step[2] + 1)])
                    for t in range(tiles):
                        instruction = dve.bn_stats(bn[:, k % 2, t, :], x_sb[:, first + t, :])
                    make(step, instruction)
                elif step[0] == "mean_var":
                    k = norm_no[step[1:]]
                    dve.wait_ge(vec_order, made[("tile_stats",) + step[1:]])
                    if k >= 2:
                        dve.wait_ge(rstd_ready, k - 1)
                    for t in range(norm_tiles[k][1]):
                        instruction = dve.bn_aggr(mean_var[:, k % 2, t, :], bn[:, k % 2, t, :])
                    make(step, instruction)
                elif step[0] in ("stats", "stats2"):
                    k = norm_no[step]
                    tiles = norm_tiles[k][1]
                    dve.wait_ge(vec_order, made[("mean_var",) + step])
                    dve.tensor_scalar(neg_mean[:, k % 2, 0:tiles], mean_var[:, k % 2, 0:tiles, 0], -1.0, None, ALU.mult)
                    dve.tensor_scalar(var_eps[:, k % 2, 0:tiles], mean_var[:, k % 2, 0:tiles, 1], EPS, None,
                                      ALU.add).then_inc(var_ready, 1)
                elif step[0] in ("normalize", "normalize2") and by_vec_norm[norm_no[("stats" + step[0][9:], step[1])]]:
                    k = norm_no[("stats" + step[0][9:], step[1])]
                    if k >= 2:
                        name, h = norms[k - 2]
                        dve.wait_ge(act_filled, act_slot[("norm" + name[5:] + "_t", h)] + 1)
                    dve.wait_ge(rstd_ready, k + 1)
                    first, tiles = norm_tiles[k]
                    for t in range(tiles):
                        dve.tensor_scalar(normed[:, k % 2, t, :], x_sb[:, first + t, :], mean_var[:, k % 2, t, 0:1],
                                          rstd[:, k % 2, t:t + 1], ALU.subtract, ALU.mult).then_inc(vec_normed, 1)
                elif step[0] == "silu":
                    dve.wait_ge(exp_c, 1)
                    link(dve.tensor_scalar(silu[:, 1:2], silu[:, 0:1], 1.0, None, ALU.add))
                    link(dve.reciprocal(silu[:, 2:3], silu[:, 1:2]))
                    link(dve.tensor_tensor(silu[:, 3:4], c_col[:, :], silu[:, 2:3], ALU.mult))
                    dve.wait_ge(const_ready, CONSTS["ones"])
                    dve.tensor_scalar(silu_wide[:, :], ones[:, :], silu[:, 3:4], None, ALU.mult).then_inc(silu_ready, 1)
                elif step[0] == "modulation":
                    dve.tensor_copy(gate_raw[:, :, :], banks[:, 1, 0:2 * D].rearrange("p (g d) -> p g d", g=2))
                    dve.tensor_copy(mod_col[:, 0:2], banks[:, 0, 0:2])
                    dve.tensor_scalar(mod_col[:, 2:4], banks[:, 0, 2:4], 1.0, None, ALU.add).then_inc(vec_drained, 1)
                elif step[0] == "gates":
                    dve.wait_ge(vec_drained, vec_slot[("modulation",)] + 1)
                    link(dve.tensor_scalar(gate_sign[:, :, :], gate_raw[:, :, :], 0.0, 2.0, ALU.is_ge, ALU.mult))
                    link(dve.tensor_scalar(gate_sign[:, :, :], gate_sign[:, :, :], -1.0, None, ALU.add))
                    link(dve.scalar_tensor_tensor(gate_size[:, :, :], gate_raw[:, :, :], -1.0, gate_raw[:, :, :],
                                                  ALU.mult, ALU.max))
                    link(dve.scalar_tensor_tensor(gates[:, :, :], gate_size[:, :, :], GATE_FLOOR, gate_sign[:, :, :],
                                                  ALU.max, ALU.mult))
                    dve.wait_ge(act_drained, act_slot[("weights",)] + 1)
                    dve.tensor_tensor(wv_gated[:, :], w_t[:, 2, :], gates[:, 0, :],
                                      ALU.mult).then_inc(gates_ready, 1)
                elif step[0] == "expert_out":
                    dve.tensor_tensor(ffn_w[:, :, :], banks[:, 0, 0:2 * D].rearrange("p (e d) -> p e d", e=2),
                                      gates[:, 1:2, :].broadcast_to([P, 2, D]), ALU.mult).then_inc(vec_drained, 1)
                elif step[0] == "project":
                    _, g, qk = step
                    dve.wait_ge(piece_ready[0], 2 * g + 2 - qk)
                    if g:
                        dve.wait_ge(piece_ready[2], 2 * g - qk)
                    dve.tensor_tensor(left[:, qk, :], banks[:, 0, :], piece[0][:, qk, g * GROUP:(g + 1) * GROUP],
                                      ALU.subtract).then_inc(vec_drained, 1)
                elif step[0] == "middle" and step[1] == 0:
                    qk = step[2]
                    dve.wait_ge(piece_ready[1], 2 - qk)
                    dve.tensor_tensor(piece[2][:, qk, 0:GROUP], left[:, qk, :], piece[1][:, qk, 0:GROUP],
                                      ALU.subtract).then_inc(piece_ready[2], 1)
                elif step[0] == "max_reduce":
                    n = step[1]
                    tiles = BLOCKS[n // 2][1]
                    dve.wait_ge(vec_drained, vec_slot[maxima_units(n)[-1]] + 1)
                    make(step, dve.tensor_reduce(neg_max[:, 0:tiles * HALF],
                                                 part_max[:, n % 2, 0:tiles, :, 0:key_chunks(n)].rearrange(
                                                     "p i e c -> p (i e) c"), AX.X, ALU.max, negate=True))
                elif step[0] in ("max_high", "max_sum"):
                    n = step[1]
                    tiles = BLOCKS[n // 2][1]
                    whole = neg_max[:, 0:tiles * HALF].rearrange("p (i e) -> p i e", e=HALF)
                    pieces = max_piece[:, n % 2, 0:tiles]
                    if step[0] == "max_high":
                        dve.wait_ge(vec_order, made[("max_reduce", n)])
                        if n >= 2:
                            dve.wait_ge(act_filled, act_slot[("max_t", n - 2)] + 1)
                        make(step, dve.tensor_copy(pieces[:, :, 0, :], whole))
                    else:
                        dve.wait_ge(vec_order, made[("max_high", n)])
                        dve.tensor_tensor(pieces[:, :, 1, :], whole, pieces[:, :, 0, :],
                                          ALU.subtract).then_inc(max_ready, 1)
                elif step[0] == "context_t":
                    n = step[1]
                    tiles = BLOCKS[n // 2][1]
                    heads = banks[:, 0, 0:tiles * P].rearrange("p (t h v) -> p t h v", t=tiles, h=HALF)
                    link(dve.reciprocal(sum_inv[:, 0:tiles, :], heads[:, :, :, HD]))
                    dve.tensor_tensor(ctx_norm[:, 0:tiles, :].rearrange("p t (h d) -> p t h d", h=HALF),
                                      heads[:, :, :, 0:HD],
                                      sum_inv[:, 0:tiles, :].unsqueeze(3).broadcast_to([P, tiles, HALF, HD]),
                                      ALU.mult).then_inc(vec_drained, 1)
                elif step[0] == "context_add":
                    n = step[1]
                    (first, tiles), feature = BLOCKS[n // 2], (n % 2) * HALF * HD
                    dve.wait_ge(vec_drained, vec_slot[("context_t", n)] + 1)
                    part = x_sb[:, first:first + tiles, feature:feature + HALF * HD]
                    make(step, dve.tensor_tensor(part, part, ctx_norm[:, 0:tiles, :], ALU.add))
                elif step[0] == "logits":
                    tiles = BLOCKS[step[1]][1]
                    if step[1]:
                        dve.wait_ge(gate_exp, step[1])
                    logits = banks[:, 0, 0:tiles * NE].rearrange("p (t e) -> p t e", e=NE)
                    link(dve.tensor_reduce(top[:, 0:tiles], logits, AX.X, ALU.max))
                    instruction = dve.tensor_tensor(shifted[:, 0:tiles, :], logits,
                                                    top[:, 0:tiles].unsqueeze(2).broadcast_to([P, tiles, NE]),
                                                    ALU.subtract)
                    instruction.then_inc(vec_drained, 1)
                elif step[0] == "gate":
                    _, g, m = step
                    ts = slice(0, BLOCKS[g][1])
                    wide = [P, BLOCKS[g][1], NE]
                    if m == 0:
                        dve.wait_ge(gate_exp, g + 1)
                        instruction = dve.tensor_reduce(gate_sum[:, ts], gate_e[:, ts, :], AX.X, ALU.add)
                    else:
                        dve.wait_ge(vec_order, made[("gate", g, m - 1)])
                    if m == 1:
                        instruction = dve.reciprocal(gate_inv[:, ts], gate_sum[:, ts])
                    elif m == 2:
                        instruction = dve.tensor_tensor(gate_p[:, ts, :], gate_e[:, ts, :],
                                                        gate_inv[:, ts].unsqueeze(2).broadcast_to(wide), ALU.mult)
                    elif m == 3:
                        dve.tensor_scalar(flags[:, ts, 0, :], gate_p[:, ts, :], TOP_P, None, ALU.is_le)
                        instruction = dve.tensor_scalar(flags[:, ts, 1, :], gate_p[:, ts, :], TOP_P, None, ALU.is_gt)
                    elif m == 4:
                        instruction = dve.tensor_reduce(count[:, ts, :], flags[:, ts, :, :], AX.X, ALU.add)
                    elif m == 5:
                        instruction = dve.tensor_tensor(expert_scale[:, ts, :], count[:, ts, :], gate_p[:, ts, 0:2],
                                                        ALU.mult)
                    make(step, instruction)
                elif step[0] == "ffn":
                    g = step[1]
                    first, tiles = BLOCKS[g]
                    dve.wait_ge(vec_order, made[("gate", g, GATE_STEPS - 1)])
                    if g >= 2:
                        dve.wait_ge(out_stored[g - 2], 16)
                    flat = banks.rearrange("p b (t e d) -> p (b t) e d", t=TG // 2, e=2)
                    for t in range(tiles):
                        instruction = dve.scalar_tensor_tensor(
                            result[:, g % 2, t, :], flat[:, t, 0, :], expert_scale[:, t, 0:1], x_sb[:, first + t, :],
                            ALU.mult, ALU.add)
                    link(instruction)
                    for t in range(tiles):
                        instruction = dve.scalar_tensor_tensor(
                            result[:, g % 2, t, :], flat[:, t, 1, :], expert_scale[:, t, 1:2], result[:, g % 2, t, :],
                            ALU.mult, ALU.add)
                        if t == tiles - 2:
                            instruction.then_inc(vec_order, 1)
                            chain[0] += 1
                            dve.wait_ge(vec_order, chain[0])
                    instruction.then_inc(vec_drained, 1)

        @block.tensor
        def _(pe):
            def wait_spread(h):
                pe.wait_ge(act_drained, act_slot[("spread", h, 0)] + 1)

            for step in steps:
                if step in act_slot:
                    bank = ps[:, banks_of[step][0], :]
                    filled = act_filled
                if step in vec_slot:
                    banks = ps[:, banks_of[step][0]:banks_of[step][-1] + 1, :]
                    filled = vec_filled
                by_act = [act_slot[s] + 1 for s in last_users[step] if s in act_slot]
                by_vec = [vec_slot[s] + 1 for s in last_users[step] if s in vec_slot]
                if by_act:
                    pe.wait_ge(act_drained, max(by_act))
                if by_vec:
                    pe.wait_ge(vec_drained, max(by_vec))
                last = None
                if step[0] == "scores":
                    _, b, e = step
                    n, j = batches[b]
                    (tile, tiles), q0 = BLOCKS[n // 2], first_query(b)
                    heads = HALF // score_slots(n)
                    if j == 0 and e == 0:
                        pe.wait_ge(max_in[n], 16 * SHIFT_ROWS)
                        if n == 0:
                            pe.wait_ge(ones_in, 16)
                    rows = ROWS + SHIFT_ROWS
                    for m in range(heads):
                        h = HALF * (n % 2) + heads * e + m
                        last = pe.matmul(bank[:, m * tiles * P + q0:(m + 1) * tiles * P],
                                         k_stack[0:rows, h, j * P:(j + 1) * P],
                                         q_stack[0:rows, h, tile * P + q0:(tile + tiles) * P],
                                         start=True, stop=True)
                elif step[0] == "maxima":
                    _, n, i, e, c = step
                    tile = BLOCKS[n // 2][0] + i
                    g = tile // TG
                    if g and i == 0:
                        pe.wait_ge(stack_in[g], 16 * 2 * NPR)
                    width = maxima_width(n, i, c)
                    for m in range(2):
                        h = HALF * (n % 2) + 2 * e + m
                        if g == 0 and i == 0:
                            wait_spread(h)
                        last = pe.matmul(banks[:, m, 0:width], q_stack[0:ROWS, h, tile * P:(tile + 1) * P],
                                         k_stack[0:ROWS, h, c * BANK:c * BANK + width],
                                         start=True, stop=c < g)
                    if c == g:
                        pe.wait_ge(const_ready, CONSTS["mask"])
                        for m in range(2):
                            last = pe.matmul(banks[:, m, width - P:width], ident_bf[:, :], mask[:, :],
                                             start=False, stop=True)
                elif step[0] == "probs_v":
                    b = step[1]
                    n, j = batches[b]
                    first, tiles = BLOCKS[n // 2]
                    q0, queries = first_query(b), tiles * P
                    pe.wait_ge(act_drained, act_slot[("scores", b, score_slots(n) - 1)] + 1)
                    if b in diagonal:
                        pe.wait_ge(masked, masks_until(b))
                    if j % TG == 0 and j // TG == first // TG:
                        pe.wait_ge(act_drained, act_slot[("values", j // TG)] + 1)
                    if j == 0 and n:
                        pe.wait_ge(ctx_copied, n)
                    for e in range(HALF):
                        last = pe.matmul(ctx_ps[VW * e:VW * e + VW, q0:queries], v_aug[:, j, HALF * (n % 2) + e, :],
                                         probs[:, b % PROB_BUFS, e, q0:queries], start=(j == 0),
                                         stop=(j == first + tiles - 1))
                    filled = pv_done
                elif step[0] == "warm":
                    pe.wait_ge(zeros_ready, 1)
                    for m in range(step[1]):
                        pe.matmul(ctx_ps[:, :], zeros[:, 0:P], zeros[:, :], start=True, stop=True)
                elif step[0] == "spread":
                    _, h, qk = step
                    pe.wait_ge(const_ready, CONSTS["spread"])
                    for m in range(3):
                        pe.wait_ge(piece_ready[m], 2 - qk)
                        last = pe.matmul(bank[0:ROWS, :], spread[:, qk, m, h].rearrange("p r d -> p (r d)"),
                                         piece[m][:, qk, 0:GROUP], start=m == 0, stop=m == 2)
                elif step[0] == "weights":
                    pe.wait_ge(const_ready, CONSTS["ident"])
                    pe.wait_ge(w_in, 16 * 5)
                    for w in range(3):
                        last = pe.transpose(bank[:, w * D:(w + 1) * D], w_sb[:, w, :], ident[:, :])
                elif step[0] == "ffn_weights":
                    pe.transpose(bank[:, 0:D], w_sb[:, 3, :], ident[:, :])
                    last = pe.transpose(bank[:, D:D + NE], gate_w[:, :], ident[0:NE, 0:NE])
                elif step[0] == "modulation":
                    pe.wait_ge(silu_ready, 1)
                    pe.wait_ge(mod_in, 16)
                    for m, s in enumerate((0, 3, 1, 4)):
                        pe.matmul(banks[:, 0, m:m + 1], wmod[:, s, :], silu[:, 3:4], start=True, stop=True)
                    for m, s in enumerate((2, 5)):
                        last = pe.matmul(banks[:, 1, m * D:(m + 1) * D], silu_wide[:, :], wmod[:, s, :],
                                         start=True, stop=True)
                elif step[0] == "expert_out":
                    pe.wait_ge(expert_in, 16)
                    pe.wait_ge(act_drained, act_slot[("ffn_weights",)] + 1)
                    for m in range(2):
                        last = pe.matmul(banks[:, 0, m * D:(m + 1) * D], expert_w[:, m, :], out_w_t[:, :],
                                         start=True, stop=True)
                elif step[0] in ("norm_t", "norm2_t"):
                    m = norm_no[("stats" + step[0][4:-2], step[1])]
                    for t in range(norm_tiles[m][1]):
                        wait_normed(pe, m, t + 1)
                        last = pe.transpose(bank[:, t * P:(t + 1) * P], normed[:, m % 2, t, :], ident[:, :])
                elif step[0] == "project":
                    _, g, qk = step
                    pe.wait_ge(act_drained, act_slot[("norm_t", g)] + 1)
                    last = pe.matmul(banks[:, 0, :], w_t[:, qk, :], h_t[:, g * GROUP:(g + 1) * GROUP],
                                     start=True, stop=True)
                elif step[0] == "values":
                    g = step[1]
                    pe.wait_ge(gates_ready, 1)
                    for t in range(TG):
                        last = pe.matmul(bank[:, t * D:(t + 1) * D], h_t[:, (TG * g + t) * P:(TG * g + t + 1) * P],
                                         wv_gated[:, :], start=True, stop=True)
                elif step[0] == "max_t":
                    n = step[1]
                    pe.wait_ge(max_ready, n + 1)
                    rows = bank.bitcast(BF16)
                    for i in range(BLOCKS[n // 2][1]):
                        last = pe.transpose(rows[0:SHIFT_ROWS * HALF, i * P:(i + 1) * P],
                                            max_piece[:, n % 2, i].rearrange("p a e -> p (a e)"), ident_bf[:, :])
                elif step[0] == "context_t":
                    n = step[1]
                    pe.wait_ge(ctx_copied, n + 1)
                    for t in range(BLOCKS[n // 2][1]):
                        last = pe.transpose(banks[:, 0, t * P:(t + 1) * P], ctx_t[:, n % 2, t * P:(t + 1) * P],
                                            ident[:, :])
                elif step[0] == "logits":
                    g = step[1]
                    pe.wait_ge(act_drained, act_slot[("norm2_t", g)] + 1)
                    for t in range(BLOCKS[g][1]):
                        last = pe.matmul(banks[:, 0, t * NE:(t + 1) * NE], h2_t[:, t * P:(t + 1) * P], gate_w_t[:, :],
                                         start=True, stop=True)
                elif step[0] == "ffn":
                    g = step[1]
                    for t in range(BLOCKS[g][1]):
                        last = pe.matmul(banks[:, t // 2, (t % 2) * 2 * D:(t % 2 + 1) * 2 * D],
                                         h2_t[:, t * P:(t + 1) * P], ffn_w[:, :, :].rearrange("p e d -> p (e d)"),
                                         start=True, stop=True)
                if last is not None:
                    last.then_inc(filled, 1)


_INS = ["L0_attn_hidden_states", "L0_attn_Wq", "L0_attn_Wk", "L0_attn_Wv", "L0_ffn_gate_W", "L0_ffn_expert_W",
        "L0_ffn_out_W", "L0_c", "L0_wmod"]


def kernel(**inputs):
    import numpy as np
    import concourse.bacc as bacc
    from concourse.bass_utils import run_bass_kernel_spmd

    nc = bacc.Bacc("TRN2", target_bir_lowering=False, num_devices=1)
    arrays, args = {}, []
    for name in _INS:
        a = np.ascontiguousarray(inputs[name])
        arrays[f"in_{name}"] = a
        args.append(nc.dram_tensor(f"in_{name}", a.shape, mybir.dt.from_np(a.dtype), kind="ExternalInput").ap())
    out = nc.dram_tensor("out_x", (1, S, D), F32, kind="ExternalOutput").ap()
    block_kernel(nc, *args, out)
    r = run_bass_kernel_spmd(nc, [arrays], core_ids=[0])
    return r.results[0]["out_x"]
```
